# Optimizing a Trainium2 kernel written in Bass

```python
import numpy as np
import jax
import jax.numpy as jnp

def _softmax(x, axis=-1):
    return jax.nn.softmax(x, axis=axis)

def _gelu(x):
    return jax.nn.gelu(x, approximate=True)

def _silu(x):
    return jax.nn.silu(x)

def _sigmoid(x):
    return jax.nn.sigmoid(x)

def _layernorm(x, axis=-1, eps=1e-05):
    m = jnp.mean(x, axis=axis, keepdims=True)
    v = jnp.var(x, axis=axis, keepdims=True)
    return (x - m) / jnp.sqrt(v + eps)

def _scatter_add(tgt, idx, src, axis=0):
    return tgt.at[idx].add(src)

def _segment_sum(src, seg, n):
    return jax.ops.segment_sum(src, seg, n)
kernel_name = 'mk_adj_resnorm_d2_adj_r2_df4b3c'

def setup_inputs(seed: int=0):
    np.random.seed(seed)
    _w = jnp.asarray

    def _rec_inputs():
        import jax
        import jax.numpy as jnp
        _gk = jax.random.key(seed)
        x = -0.0002928 + 1 * jax.random.normal(jax.random.fold_in(_gk, 1), (4096, 256), jnp.float32)
        _a = jax.random.bernoulli(jax.random.fold_in(_gk, 2), 0.00195312, (4096, 4096))
        adj = _a.astype(jnp.int32)
        return (x, adj)
    x, adj = _rec_inputs()

    def _L0_gnn_setup():
        import jax, jax.numpy as jnp
        import numpy as np
        EPS = 1e-08
        key = jax.random.key(seed)
        k1, k2, k3 = jax.random.split(key, 3)
        N, IN_DIM, OUT_DIM = (4096, 256, 256)
        h = jax.random.normal(k1, (N, IN_DIM), dtype=jnp.float32)
        adj = jax.random.randint(k2, (N, N), 0, 2, dtype=jnp.int32)
        W = jax.random.normal(k3, (OUT_DIM, IN_DIM), dtype=jnp.float32) * (1.0 / np.sqrt(IN_DIM))
        return {'h': h, 'adj': adj, 'W': W}
    _L0_gnn_all = _L0_gnn_setup()
    _L0_gnn_in = {k: v for k, v in _L0_gnn_all.items() if k in ('W',)}
    del _L0_gnn_all

    def _L1_gnn_setup():
        import jax, jax.numpy as jnp
        import numpy as np
        N, D_IN, D_OUT = (4096, 256, 256)
        key = jax.random.key(seed)
        ks = jax.random.split(key, 8)
        scale_in = 1.0 / np.sqrt(D_IN)
        scale_cat = 1.0 / np.sqrt(2 * D_OUT)
        return {'x': jax.random.normal(ks[0], (N, D_IN), dtype=jnp.float32), 'adj': jax.random.randint(ks[1], (N, N), 0, 2, dtype=jnp.int32), 'W_self': jax.random.uniform(ks[2], (D_IN, D_OUT), jnp.float32, -scale_in, scale_in), 'b_self': jax.random.uniform(ks[3], (D_OUT,), jnp.float32, -scale_in, scale_in), 'W_nb': jax.random.uniform(ks[4], (D_IN, D_OUT), jnp.float32, -scale_in, scale_in), 'b_nb': jax.random.uniform(ks[5], (D_OUT,), jnp.float32, -scale_in, scale_in), 'W_comb': jax.random.uniform(ks[6], (2 * D_OUT, D_OUT), jnp.float32, -scale_cat, scale_cat), 'b_comb': jax.random.uniform(ks[7], (D_OUT,), jnp.float32, -scale_cat, scale_cat)}
    _L1_gnn_all = _L1_gnn_setup()
    _L1_gnn_in = {k: v for k, v in _L1_gnn_all.items() if k in ('W_self', 'b_self', 'W_nb', 'b_nb', 'W_comb', 'b_comb')}
    del _L1_gnn_all
    return {'x': x, 'adj': adj, 'L0_gnn_W': _L0_gnn_in['W'], 'L1_gnn_W_self': _L1_gnn_in['W_self'], 'L1_gnn_b_self': _L1_gnn_in['b_self'], 'L1_gnn_W_nb': _L1_gnn_in['W_nb'], 'L1_gnn_b_nb': _L1_gnn_in['b_nb'], 'L1_gnn_W_comb': _L1_gnn_in['W_comb'], 'L1_gnn_b_comb': _L1_gnn_in['b_comb']}

def reference(x, adj, L0_gnn_W, L1_gnn_W_self, L1_gnn_b_self, L1_gnn_W_nb, L1_gnn_b_nb, L1_gnn_W_comb, L1_gnn_b_comb):
    import jax
    import jax.numpy as jnp

    def _L0_gnn_ref(h, adj, W):
        import jax, jax.numpy as jnp
        import numpy as np
        EPS = 1e-08
        Wh = h @ W.T
        N = Wh.shape[0]
        norms = jnp.linalg.norm(Wh, axis=1, keepdims=True)
        sim = Wh @ Wh.T / (norms * norms.T + EPS)
        mask = (adj > 0) | jnp.eye(N, dtype=bool)
        sim_masked = jnp.where(mask, sim, -jnp.inf)
        alpha = jax.nn.softmax(sim_masked, axis=1)
        return alpha @ Wh

    def _L1_gnn_ref(x, adj, W_self, b_self, W_nb, b_nb, W_comb, b_comb):
        import jax, jax.numpy as jnp
        import numpy as np
        N, D_IN, D_OUT = (4096, 256, 256)
        mask = (adj > 0).astype(x.dtype)
        deg = jnp.sum(mask, axis=1, keepdims=True)
        agg = mask @ x / jnp.maximum(deg, 1.0)
        self_f = x @ W_self + b_self
        nb_f = agg @ W_nb + b_nb
        combined = jnp.concatenate([self_f, nb_f], axis=-1)
        out = combined @ W_comb + b_comb
        return jax.nn.relu(out)
    x = _layernorm(x + _L0_gnn_ref(x, adj, L0_gnn_W), axis=-1)
    x = _layernorm(x + _L1_gnn_ref(x, adj, L1_gnn_W_self, L1_gnn_b_self, L1_gnn_W_nb, L1_gnn_b_nb, L1_gnn_W_comb, L1_gnn_b_comb), axis=-1)
    return x

_drawn_inputs = setup_inputs


def setup_inputs(seed=0):
    import zlib

    import numpy as np

    out = dict(_drawn_inputs(seed))
    spreads = {}
    factors = {'L1_gnn_b_self': 6.224, 'L1_gnn_b_nb': 5.27, 'L1_gnn_b_comb': 3.169}
    for name, (base, spread) in spreads.items():
        noise = np.random.default_rng([zlib.crc32(name.encode()), seed]).standard_normal(out[name].shape)
        drawn = base * np.exp(spread * noise) if base else spread * noise
        out[name] = jnp.asarray(drawn.astype(out[name].dtype))
    for name, factor in factors.items():
        out[name] = (out[name] * factor).astype(out[name].dtype)
    return out
```

```python
import concourse.bass as bass
from concourse import mybir
from contextlib import ExitStack
import math

N, D, P = 4096, 256, 128
KD = D // P
NT = N // P
SUB = 4
SW = SUB * P
NS = N // SW
BITS = 8
NC = NT // BITS
UNITS = BITS // 2
UPS = NC * UNITS
HALF = N // 2
VW = 2 * D + 2
LOW = D + 2
EPS_SIM = 1e-8
EPS_LN = 1e-5
SIM_SCALE = 1024.0
VAL_TOP = 8192.0
X1_SCALE = 2048.0
MASK_ONE = 2.0
EXP_BIAS = -1.0 + 13.0 * math.log(2.0)


def gnn_kernel(nc, x, adj, w0, w_self, b_self, w_nb, b_nb, w_comb, b_comb, out):
    f32, f16, bf16 = mybir.dt.float32, mybir.dt.float16, mybir.dt.bfloat16
    u16, u8, i32 = mybir.dt.uint16, mybir.dt.uint8, mybir.dt.int32
    ALU, ACT, AX = mybir.AluOpType, mybir.ActivationFunctionType, mybir.AxisListType
    ds = bass.ds

    ctx = ExitStack()
    with ctx:
        def sb(name, shape, dt):
            return ctx.enter_context(nc.sbuf_tensor(name, shape, dt))

        def sem(name):
            return ctx.enter_context(nc.semaphore(name))

        X = sb("X", [P, NT, D], f32)
        similar = sb("similar", [P, 2, KD, N], f16)
        values = sb("values", [P, NT, VW], f16)
        words = sb("words", [P, NS, NC, SW], u16)
        mask = sb("mask", [P, BITS, SW], u16)
        adj_in = sb("adj_in", [P, 2, HALF], i32)
        bits = sb("bits", [P, 2, HALF], bf16)
        pair = sb("pair", [P, 2, 2, SW], bf16)
        quad = sb("quad", [P, 2, SW], bf16)
        row_words = sb("row_words", [P, SUB, SW], bf16)
        Ph = sb("Ph", [P, UNITS, 2, SW], f16)
        Pl = sb("Pl", [P, UNITS, 2, SW], f16)
        M1 = sb("M1", [P, KD, D], f32)
        M2 = sb("M2", [P, KD, D], f32)
        bias = sb("bias", [P, D], f32)
        ident32 = sb("ident32", [P, P], f32)
        ident16 = sb("ident16", [P, P], f16)
        identb = sb("identb", [P, P], bf16)
        diag2 = sb("diag2", [P, P], f16)
        sign_junk = sb("sign_junk", [P, HALF], u8)
        bcol = sb("bcol", [P, 2 * KD], f32)
        norm2 = sb("norm2", [P, NT], f32)
        rnorm = sb("rnorm", [P, SUB], f32)
        mixed = sb("mixed", [P, SUB, D], f32)
        minus_half = sb("minus_half", [P, SUB], f32)
        plus_half = sb("plus_half", [P, 1], f32)
        big = sb("big", [P, 4], f32)
        exp_bias = sb("exp_bias", [P, 1], f32)
        degree = sb("degree", [P, NT, 2], f32)
        rdeg = sb("rdeg", [P, NT], f32)
        rsum = sb("rsum", [P, SUB], f32)
        stats = sb("stats", [P, SUB, 6], f32)
        mean_sum, mean_gap, gap2, squares, mean = (
            sb(n, [P, SUB], f32) for n in ("mean_sum", "mean_gap", "gap2", "squares", "mean"))
        rstd = sb("rstd", [P, SUB], f32)
        stage = sb("stage", [P, SUB, D], f32)

        Wh = words[:, :, :, :].rearrange("p s c w -> p (s c w)").bitcast(f32).rearrange(
            "p (t d) -> p t d", d=D)
        wst = Ph[:, :, :, :].rearrange("p q k w -> p (q k w)").bitcast(f32).rearrange(
            "p (a d) -> p a d", d=D)
        w0_in, wself_in, wnb_in, wcomb_in = (
            wst[:, 0:2, :], wst[:, 2:4, :], wst[:, 4:6, :], values[:, 0:4, 0:2 * D].bitcast(f32))
        wstT = Pl[:, :, :, :].rearrange("p q k w -> p (q k w)").bitcast(f32).rearrange(
            "p (a d) -> p a d", d=D)
        w0T, wselfT, wnbT = wstT[:, 0:2, :], wstT[:, 2:4, :], wstT[:, 4:6, :]
        bcomb_in = wst[:, 6, :]
        bcast = wstT[:, 6:8, :].rearrange("p a (b n) -> p (a b) n", n=P)
        mask_flat = mask[:, :, :].rearrange("p b w -> p (b w)")
        xT = mask_flat[:, 0:4 * SW].bitcast(f32).rearrange("p (t k n) -> p t k n", t=SUB, k=KD)
        unit = mask_flat[:, 4 * SW:8 * SW].bitcast(f16).rearrange("p (h t d) -> p h t d", h=2, t=SUB)
        mask16 = mask_flat.bitcast(f16).rearrange("p (b w) -> p b w", w=SW)
        mask_pairs = mask_flat.bitcast(f16).rearrange("p (q w) -> p q w", w=2 * SW)
        x1s = values
        late = similar[:, :, :, :].rearrange("p h k n -> p (h k n)").bitcast(f32)
        aggT = late[:, 0:1024].rearrange("p (k n) -> p k n", k=KD)
        x1T = late[:, 1024:2048].rearrange("p (t k n) -> p t k n", t=SUB, k=KD)
        feat = late[:, 2048:3072].rearrange("p (t d) -> p t d", d=D)
        result = late[:, 3072:4096].rearrange("p (t d) -> p t d", d=D)

        ps = ctx.enter_context(nc.psum_tensor("ps", [P, 8, 512], f32))
        ps_flat = ps[:, :, :].rearrange("p b w -> p (b w)")
        sim_ps = [ps_flat[:, 0:1024], ps_flat[:, 1024:2048]]
        word_ps = sim_ps[0].bitcast(bf16)
        out_ps = ps[:, 4:8, :]

        x_first, x_rest, w_in, wc_in = sem("x_first"), sem("x_rest"), sem("w_in"), sem("wc_in")
        consts, staged, ln_done = sem("consts"), sem("staged"), sem("layernorm_done")
        pool_step = sem("pool_step")
        w_t, w_tc = sem("w_transposed"), sem("w_copied")
        bc_done, fused, fused_copied = sem("bias_columns"), sem("weights_fused"), sem("fused_copied")
        xt_done, xt_copied = sem("x_transposed"), sem("x_copied")
        wh_done, wh_copied, sq_done = sem("wh_done"), sem("wh_copied"), sem("squares_done")
        n2_done, rn_done = sem("norm2_done"), sem("rnorm_done")
        unit_hi, unit_done = sem("unit_high"), sem("unit_done")
        ut_done, ut_copied = sem("unit_transposed"), sem("unit_copied")
        top_done, max_done, all_max, scale_done, vscale_done = (
            sem("row_max_done"), sem("max_done"), sem("all_max"), sem("scale_done"), sem("vscale_done"))
        vh_done, vl_done = sem("values_high"), sem("values_low")
        adj_ready = [sem("adj_ready0"), sem("adj_ready1")]
        bits_done = [sem("bits_done0"), sem("bits_done1")]
        deg_done = [sem("deg_done0"), sem("deg_done1")]
        pairs_done, quads_done, row_words_done = sem("pairs_done"), sem("quads_done"), sem("row_words_done")
        words_t, words_stored = sem("words_transposed"), sem("words_stored")
        unpacked, diag_done = sem("unpacked"), sem("diag_done")
        sims, exps, masked, highs, lows, attended = (
            sem("sims"), sem("exps"), sem("masked"), sem("highs"), sem("lows"), sem("attended"))
        rs_done, rs_scaled, attn_read = sem("rsum_done"), sem("rsum_scaled"), sem("attn_read")
        st_done, parts_done, var_done, rstd_done = (
            sem("stats_done"), sem("moment_parts"), sem("variance_done"), sem("rstd_done"))
        deg_sum, deg_max, rdeg_done = sem("deg_sum"), sem("deg_max"), sem("rdeg_done")
        x1_hi, x1_split = sem("x1_high"), sem("x1_split")
        mask_ready, mask_used = sem("mask_ready"), sem("mask_used")
        agg_copied = sem("agg_copied")
        x1t_done, x1t_copied = sem("x1_transposed"), sem("x1t_copied")
        feat_done, feat_b, feat_sum, feat_res = (
            sem("features_done"), sem("features_biased"), sem("features_summed"), sem("features_residual"))
        stored = sem("stored")

        block = ctx.enter_context(nc.Block())

        def since(eng, s, v):
            if not (isinstance(v, int) and v <= 0):
                eng.wait_ge(s, v)

        @block.sync
        def _(sp):
            xv = x.rearrange("(t p) d -> p t d", p=P)
            sp.dma_start(X[:, 0:SUB, :], xv[:, 0:SUB, :]).then_inc(x_first, 16)
            sp.dma_start(X[:, SUB:NT, :], xv[:, SUB:NT, :]).then_inc(x_rest, 16)
            for h in range(2):
                sp.dma_start(adj_in[:, h, :], adj[0:P, h * HALF:(h + 1) * HALF]).then_inc(adj_ready[h], 16)
            with sp.Fori(1, NT) as t:
                for h in range(2):
                    sp.wait_ge(bits_done[h], t)
                    sp.dma_start(adj_in[:, h, :], adj[ds(t * P, P), h * HALF:(h + 1) * HALF]).then_inc(
                        adj_ready[h], 16)
            def stage_x1(s):
                sp.dma_start(stage[:, :, :], X[:, ds(s * SUB, SUB), :]).then_inc(staged, 16)

            def store(s):
                sp.wait_ge(ln_done, NS + s + 1)
                sp.dma_start(out[ds(s * SW, SW), :].rearrange("(t p) d -> p t d", p=P),
                             result).then_inc(stored, 16)

            sp.wait_ge(ln_done, NS)
            stage_x1(0)
            with sp.Fori(1, NS) as s:
                sp.wait_ge(x1t_done, s)
                stage_x1(s)
                store(s - 1)
            store(NS - 1)
            sp.wait_ge(stored, 16 * NS)

        @block.gpsimd
        def _(pool):
            for t in (ident32, ident16, identb, diag2):
                nc.gpsimd.memset(t[:], 0.0)
            nc.gpsimd.memset(minus_half[:], -0.5)
            nc.gpsimd.memset(plus_half[:], 0.5)
            nc.gpsimd.memset(exp_bias[:], EXP_BIAS).then_inc(pool_step, 1)
            pool.wait_ge(pool_step, 1)
            for t, one in ((ident32, 1.0), (ident16, 1.0), (identb, 1.0), (diag2, MASK_ONE)):
                last = nc.gpsimd.affine_select(out=t[:], in_=t[:], compare_op=ALU.not_equal, fill=one, base=0,
                                               pattern=[[-1, P]], channel_multiplier=1)
            last.then_inc(consts, 1)

            with pool.Fori(0, NS) as g:
                pool.wait_ge(n2_done, g + 1)
                nc.gpsimd.tensor_tensor(out=rnorm[:], in0=rnorm[:], in1=minus_half[:], op=ALU.pow).then_inc(rn_done, 1)
            pool.wait_ge(max_done, 1)
            nc.gpsimd.partition_all_reduce(big[:, 1:2], big[:, 0:1], P, bass.bass_isa.ReduceOp.max).then_inc(all_max, 1)
            pool.wait_ge(all_max, 1)
            nc.gpsimd.tensor_tensor(out=big[:, 2:3], in0=big[:, 1:2], in1=minus_half[:, 0:1], op=ALU.pow)
            nc.gpsimd.tensor_tensor(out=big[:, 3:4], in0=big[:, 1:2], in1=plus_half[:], op=ALU.pow).then_inc(
                scale_done, 1)
            with pool.Fori(0, 2 * NS) as at:
                pool.wait_ge(var_done, at + 1)
                nc.gpsimd.tensor_tensor(out=rstd[:], in0=rstd[:], in1=minus_half[:], op=ALU.pow).then_inc(
                    rstd_done, 1)

        @block.tensor
        def _(pe):
            pe.wait_ge(consts, 1)
            pe.wait_ge(w_in, 16 * 3)
            for i, w in enumerate((w0_in, wself_in, wnb_in)):
                for ko in range(KD):
                    for ki in range(KD):
                        last = nc.tensor.transpose(ps[:, i, ki * D + ko * P:ki * D + (ko + 1) * P],
                                                   w[:, ko, ki * P:(ki + 1) * P], ident32[:])
            last.then_inc(w_t, 1)

            pe.wait_ge(w_tc, 1)
            pe.wait_ge(wc_in, 16 * 6)
            pe.wait_ge(bc_done, 1)
            for i, wT in enumerate((wselfT, wnbT)):
                for kd in range(KD):
                    for km in range(KD):
                        nc.tensor.matmul(ps[:, 3 + i, kd * D:(kd + 1) * D], wT[:, km, kd * P:(kd + 1) * P],
                                         wcomb_in[:, KD * i + km, :], start=(km == 0), stop=(km == KD - 1))
            for k in range(2 * KD):
                last = nc.tensor.matmul(ps[:, 5, 0:D], bcast[:, k, :], wcomb_in[:, k, :],
                                        start=(k == 0), stop=(k == 2 * KD - 1))
            last.then_inc(fused, 1)

            def transpose_x(g):
                since(pe, xt_copied, g)
                pe.wait_ge(staged, 16 * g + 16)
                for t in range(SUB):
                    for k in range(KD):
                        at = (t * KD + k) * P
                        last = nc.tensor.transpose(ps_flat[:, at:at + P],
                                                   stage[:, t, k * P:(k + 1) * P], ident32[:])
                last.then_inc(xt_done, 1)

            def project(g):
                pe.wait_ge(xt_copied, g + 1)
                since(pe, wh_copied, g)
                for t in range(SUB):
                    for k in range(KD):
                        last = nc.tensor.matmul(ps_flat[:, 1024 + t * D:1024 + (t + 1) * D], xT[:, t, k, :],
                                                w0T[:, k, :], start=(k == 0), stop=(k == KD - 1))
                last.then_inc(wh_done, 1)

            def transpose_unit(g):
                pe.wait_ge(unit_done, g + 1)
                since(pe, ut_copied, g)
                dst = ps_flat[:, 3072:4096].bitcast(f16)
                for h in range(2):
                    for k in range(KD):
                        for t in range(SUB):
                            at = (h * KD + k) * SW + t * P
                            last = nc.tensor.transpose(dst[:, at:at + P], unit[:, h, t, k * P:(k + 1) * P],
                                                       ident16[:])
                last.then_inc(ut_done, 1)

            pe.wait_ge(fused_copied, 2)
            transpose_x(0)
            transpose_x(1)
            project(0)
            with pe.Fori(1, NS - 1) as g:
                transpose_x(g + 1)
                project(g)
                transpose_unit(g - 1)
            project(NS - 1)
            transpose_unit(NS - 2)
            transpose_unit(NS - 1)

            def similarities(s, c, q):
                n = UPS * s + UNITS * c + q
                since(pe, lows, n - 1)
                for kk in range(2):
                    jb = NC * (2 * q + kk) + c
                    terms = [(hj, hi, k) for hj, hi in ((0, 0), (0, 1), (1, 0)) for k in range(KD)]
                    for i, (hj, hi, k) in enumerate(terms):
                        last = nc.tensor.matmul(sim_ps[q % 2][:, kk * SW:(kk + 1) * SW],
                                                similar[:, hj, k, ds(jb * P, P)],
                                                similar[:, hi, k, ds(s * SW, SW)],
                                                start=(i == 0), stop=(i == len(terms) - 1))
                last.then_inc(sims, 1)

            def attend(s, c, q):
                n = UPS * s + UNITS * c + q
                first = isinstance(c, int) and c == 0 and q == 0
                end = isinstance(c, int) and c == NC - 1 and q == UNITS - 1
                pe.wait_ge(lows, n + 1)
                if first:
                    since(pe, attn_read, s)
                for kk in range(2):
                    jb = NC * (2 * q + kk) + c
                    row = values[:, ds(jb, 1), :].rearrange("p o w -> p (o w)")
                    for t in range(SUB):
                        hi = Ph[:, q, kk, t * P:(t + 1) * P]
                        lo = Pl[:, q, kk, t * P:(t + 1) * P]
                        nc.tensor.matmul(out_ps[:, t, 0:D + 1], hi, row[:, 0:D + 1],
                                         start=first and kk == 0, stop=False, skip_group_check=True)
                        nc.tensor.matmul(out_ps[:, t, 0:D], hi, row[:, LOW:LOW + D],
                                         start=False, stop=False, skip_group_check=True)
                        last = nc.tensor.matmul(out_ps[:, t, 0:D + 1], lo, row[:, 0:D + 1],
                                                start=False, stop=end and kk == 1, skip_group_check=True)
                last.then_inc(attended, 1)

            def transpose_words(s):
                pe.wait_ge(row_words_done, SUB * s + SUB)
                since(pe, lows, UPS * s - 1)
                for t in range(SUB):
                    for c in range(NC):
                        last = nc.tensor.transpose(word_ps[:, c * SW + t * P:c * SW + (t + 1) * P],
                                                   row_words[:, t, c * P:(c + 1) * P], identb[:])
                last.then_inc(words_t, 1)

            def attention_tile(s, begin):
                transpose_words(s)
                if begin:
                    pe.wait_ge(ut_copied, NS)
                    pe.wait_ge(vl_done, NS)
                else:
                    attend(s - 1, NC - 1, UNITS - 2)
                pe.wait_ge(words_stored, s + 1)
                similarities(s, 0, 0)
                if not begin:
                    attend(s - 1, NC - 1, UNITS - 1)
                similarities(s, 0, 1)
                for q in range(2, UNITS):
                    similarities(s, 0, q)
                    attend(s, 0, q - 2)
                with pe.Fori(1, NC) as c:
                    for q in range(UNITS):
                        similarities(s, c, q)
                        attend(s, c - 1 if q < 2 else c, (q - 2) % UNITS)

            attention_tile(0, True)
            with pe.Fori(1, NS) as s:
                attention_tile(s, False)
            for q in (UNITS - 2, UNITS - 1):
                attend(NS - 1, NC - 1, q)

            def aggregate(s, c):
                first = isinstance(c, int) and c == 0
                end = isinstance(c, int) and c == NC - 1
                for b in range(BITS):
                    pe.wait_ge(mask_ready, BITS * (NC * s + c) + b + 1)
                    for k in range(KD):
                        for h in range(2):
                            jb = NC * b + c
                            at = (LOW if h else 0) + k * P
                            last = nc.tensor.matmul(ps[:, k, :],
                                                    x1s[:, ds(jb, 1), at:at + P].rearrange("p o n -> p (o n)"),
                                                    mask16[:, b, :],
                                                    start=first and b == 0 and h == 0,
                                                    stop=end and b == BITS - 1 and h == 1, skip_group_check=True)
                    last.then_inc(mask_used, 1)

            def transpose_x1(s):
                since(pe, x1t_copied, s)
                pe.wait_ge(staged, 16 * (NS + s + 1))
                for t in range(SUB):
                    for k in range(KD):
                        at = 1024 + (t * KD + k) * P
                        last = nc.tensor.transpose(
                            ps_flat[:, at:at + P],
                            stage[:, t, k * P:(k + 1) * P], ident32[:])
                last.then_inc(x1t_done, 1)

            def features(s):
                pe.wait_ge(x1t_copied, s + 1)
                pe.wait_ge(agg_copied, 2 * s + 2)
                since(pe, feat_sum, s)
                for t in range(SUB):
                    for k in range(KD):
                        nc.tensor.matmul(ps[:, 4 + t, 0:D], x1T[:, t, k, :], M1[:, k, :],
                                         start=(k == 0), stop=(k == KD - 1))
                    for k in range(KD):
                        last = nc.tensor.matmul(ps[:, 4 + t, D:2 * D], aggT[:, k, t * P:(t + 1) * P], M2[:, k, :],
                                                start=(k == 0), stop=(k == KD - 1))
                last.then_inc(feat_done, 1)

            def layer_tile(s, begin):
                if not begin:
                    pe.wait_ge(agg_copied, 2 * s)
                else:
                    pe.wait_ge(x1_split, 1)
                aggregate(s, 0)
                if not begin:
                    features(s - 1)
                else:
                    pe.wait_ge(x1_split, NC)
                with pe.Fori(1, NC - 1) as c:
                    aggregate(s, c)
                aggregate(s, NC - 1)
                transpose_x1(s)

            layer_tile(0, True)
            with pe.Fori(1, NS) as s:
                layer_tile(s, False)
            features(NS - 1)

        @block.scalar
        def _(act):
            def rows(w):
                return w.rearrange("(k p) d -> p k d", p=P)
            for dst, w in ((w0_in, w0), (wself_in, w_self), (wnb_in, w_nb)):
                act.dma_start(dst, rows(w)).then_inc(w_in, 16)
            act.dma_start(wcomb_in, rows(w_comb)).then_inc(wc_in, 16)
            for i, b in enumerate((b_self, b_nb)):
                for k in range(KD):
                    act.dma_start(bcol[:, KD * i + k:KD * i + k + 1],
                                  b[k * P:(k + 1) * P].rearrange("(p o) -> p o", o=1)).then_inc(wc_in, 16)
            act.dma_start(bcomb_in, b_comb.rearrange("(o d) -> o d", o=1).broadcast_to([P, D])).then_inc(wc_in, 16)

            act.wait_ge(w_t, 1)
            nc.scalar.copy(wstT[:, 2:6, :], ps[:, 1:3, :].rearrange("p i (k d) -> p (i k) d", k=KD)).then_inc(w_tc, 1)
            act.wait_ge(fused, 1)
            nc.scalar.copy(M1[:, :, :], ps[:, 3, :].rearrange("p (k d) -> p k d", k=KD))
            nc.scalar.copy(M2[:, :, :], ps[:, 4, :].rearrange("p (k d) -> p k d", k=KD)).then_inc(fused_copied, 1)

            def keep_wh(g):
                act.wait_ge(wh_done, g + 1)
                wh = Wh[:, ds(g * SUB, SUB), :]
                nc.scalar.copy(wh, ps_flat[:, 1024:2048].rearrange("p (t d) -> p t d", d=D)).then_inc(wh_copied, 1)
                act.wait_ge(wh_copied, g + 1)
                for t in range(SUB):
                    last = nc.scalar.activation(sign_junk[:, t * D:(t + 1) * D],
                                                Wh[:, ds(g * SUB + t, 1), :].rearrange("p o d -> p (o d)"),
                                                ACT.Square, accum_out=norm2[:, ds(g * SUB + t, 1)])
                last.then_inc(sq_done, 1)

            def keep_unit(g):
                act.wait_ge(ut_done, g + 1)
                nc.scalar.copy(similar[:, :, :, ds(g * SW, SW)].rearrange("p h k n -> p (h k) n"),
                               ps_flat[:, 3072:4096].bitcast(f16).rearrange("p (a n) -> p a n", a=2 * KD)).then_inc(
                                   ut_copied, 1)

            def count_degree(tile, h, squared=None):
                act.wait_ge(bits_done[h], tile + 1)
                act.wait_ge(sq_done, NS if squared is None else squared)
                since(act, deg_done[0], tile + (1 if h else 0))
                since(act, deg_done[1], tile)
                nc.scalar.activation(sign_junk[:], bits[:, h, :], ACT.Sign,
                                     accum_out=degree[:, ds(tile, 1), h:h + 1].rearrange("p o h -> p (o h)")
                                     ).then_inc(deg_done[h], 1)

            def stage_x(g):
                since(act, xt_done, g)
                act.dma_start(stage[:, :, :], X[:, ds(g * SUB, SUB), :]).then_inc(staged, 16)

            act.wait_ge(x_first, 16)
            stage_x(0)
            act.wait_ge(x_rest, 16)
            stage_x(1)
            stage_x(2)
            keep_wh(0)
            with act.Fori(1, NS - SUB - 1) as g:
                stage_x(g + 2)
                keep_wh(g)
                keep_unit(g - 1)
            with act.Fori(NS - SUB - 1, NS - 2) as g:
                stage_x(g + 2)
                keep_wh(g)
                keep_unit(g - 1)
                for h in range(2):
                    count_degree(g - (NS - SUB - 1), h, g + 1)
            keep_wh(NS - 2)
            keep_unit(NS - 3)
            for h in range(2):
                count_degree(SUB - 1, h, NS - 1)
            keep_wh(NS - 1)
            keep_unit(NS - 2)
            keep_unit(NS - 1)
            act.wait_ge(vscale_done, 1)
            with act.Fori(0, NS) as g:
                nc.scalar.activation(values[:, ds(g * SUB, SUB), 0:D], Wh[:, ds(g * SUB, SUB), :], ACT.Copy,
                                     scale=big[:, 2:3]).then_inc(vh_done, 1)
            def unit_exps(s, c, q):
                n = UPS * s + UNITS * c + q
                act.wait_ge(sims, n + 1)
                nc.scalar.activation(sim_ps[q % 2], sim_ps[q % 2], ACT.Exp, bias=exp_bias[:],
                                     scale=1.0 / SIM_SCALE ** 2).then_inc(exps, 1)
                act.wait_ge(masked, n + 1)
                since(act, attended, n - (UNITS - 1))
                nc.scalar.copy(Ph[:, q, :, :].rearrange("p k w -> p (k w)"), sim_ps[q % 2]).then_inc(highs, 1)

            def iteration(s, c, pack):
                for q in range(UNITS):
                    unit_exps(s, c, q)
                    if pack and q % 2:
                        count_degree(SUB * (s + 1) + c, q // 2)

            def exps_tile(s, pack):
                act.wait_ge(words_t, s + 1)
                if isinstance(s, int) and s == 0:
                    act.wait_ge(vl_done, NS)
                nc.scalar.copy(words[:, ds(s, 1), :, :].rearrange("p o c w -> p (o c w)"), word_ps).then_inc(
                    words_stored, 1)
                iteration(s, 0, pack)
                with act.Fori(1, NC) as c:
                    iteration(s, c, pack)

            exps_tile(0, True)
            with act.Fori(1, NS - 1) as s:
                exps_tile(s, True)
            exps_tile(NS - 1, False)

            with act.Fori(0, NS) as s:
                act.wait_ge(mask_used, BITS * NC * (s + 1))
                since(act, feat_done, s)
                nc.scalar.mul(aggT[:, 0, :], ps[:, 0, :], 1.0 / (MASK_ONE * X1_SCALE)).then_inc(agg_copied, 1)
                act.wait_ge(x1t_done, s + 1)
                nc.scalar.copy(x1T, ps_flat[:, 1024:2048].rearrange("p (t k n) -> p t k n", t=SUB, k=KD)).then_inc(
                    x1t_copied, 1)

        @block.vector
        def _(dve):
            dve.wait_ge(w_t, 1)
            nc.vector.tensor_copy(w0T, ps[:, 0, :].rearrange("p (k d) -> p k d", k=KD))
            dve.wait_ge(wc_in, 16 * 6)
            dve.wait_ge(consts, 1)
            for k in range(2 * KD):
                last = nc.vector.tensor_scalar(bcast[:, k, :], ident32[:], 0.0, bcol[:, k:k + 1], ALU.mult, ALU.add)
            last.then_inc(bc_done, 1)
            dve.wait_ge(fused, 1)
            nc.vector.tensor_tensor(out=bias[:], in0=ps[:, 5, 0:D], in1=bcomb_in, op=ALU.add).then_inc(
                fused_copied, 1)
            nc.vector.memset(values[:, :, D:D + 2], 1.0)

            def copy_xt(g):
                dve.wait_ge(xt_done, g + 1)
                since(dve, wh_done, g)
                nc.vector.tensor_copy(xT, ps_flat[:, 0:1024].rearrange("p (t k n) -> p t k n", t=SUB, k=KD)).then_inc(
                    xt_copied, 1)

            def guard_norms(g):
                dve.wait_ge(sq_done, g + 1)
                since(dve, unit_done, g)
                nc.vector.tensor_scalar(rnorm[:], norm2[:, ds(g * SUB, SUB)], EPS_SIM, 1.0 / SIM_SCALE ** 2,
                                        ALU.add, ALU.mult).then_inc(n2_done, 1)

            def split_units(g):
                dve.wait_ge(rn_done, g + 1)
                since(dve, ut_done, g)
                for t in range(SUB):
                    row = Wh[:, ds(g * SUB + t, 1), :].rearrange("p o d -> p (o d)")
                    last = nc.vector.tensor_scalar(unit[:, 0, t, :], row, rnorm[:, t:t + 1], None, ALU.mult)
                last.then_inc(unit_hi, 1)
                dve.wait_ge(unit_hi, g + 1)
                for t in range(SUB):
                    row = Wh[:, ds(g * SUB + t, 1), :].rearrange("p o d -> p (o d)")
                    last = nc.vector.scalar_tensor_tensor(unit[:, 1, t, :], row, rnorm[:, t:t + 1],
                                                          unit[:, 0, t, :], ALU.mult, ALU.subtract)
                last.then_inc(unit_done, 1)

            def take_bits(tile, h):
                dve.wait_ge(adj_ready[h], 16 * tile + 16)
                since(dve, deg_done[h], tile)
                since(dve, pairs_done, 2 * tile)
                for r in range(BITS // 2):
                    last = nc.vector.tensor_scalar(bits[:, h, r * SW:(r + 1) * SW], adj_in[:, h, r * SW:(r + 1) * SW],
                                                   0, float(2 ** (BITS // 2 * h + r)), ALU.is_gt, ALU.mult)
                last.then_inc(bits_done[h], 1)

            def sum_bits(tile, h):
                dve.wait_ge(bits_done[h], tile + 1)
                since(dve, quads_done, 2 * tile)
                nc.vector.tensor_tensor(out=pair[:, h, :, :].rearrange("p a w -> p (a w)"),
                                        in0=bits[:, h, 0:HALF // 2], in1=bits[:, h, HALF // 2:HALF],
                                        op=ALU.add).then_inc(pairs_done, 1)
                dve.wait_ge(pairs_done, 2 * tile + h + 1)
                since(dve, row_words_done, tile)
                nc.vector.tensor_tensor(out=quad[:, h, :], in0=pair[:, h, 0, :], in1=pair[:, h, 1, :],
                                        op=ALU.add).then_inc(quads_done, 1)

            def join_halves(s, t):
                tile = SUB * s + t
                dve.wait_ge(quads_done, 2 * tile + 2)
                since(dve, words_t, s)
                nc.vector.tensor_tensor(out=row_words[:, ds(t, 1), :].rearrange("p o w -> p (o w)"),
                                        in0=quad[:, 0, :], in1=quad[:, 1, :], op=ALU.add).then_inc(row_words_done, 1)

            def pack(s, t, step):
                if step % 2 == 0:
                    take_bits(SUB * s + t, step // 2)
                else:
                    sum_bits(SUB * s + t, step // 2)
                    if step == 3:
                        join_halves(s, t)

            copy_xt(0)
            with dve.Fori(0, NS - SUB - 1) as g:
                copy_xt(g + 1)
                guard_norms(g)
                split_units(g)
            with dve.Fori(NS - SUB - 1, NS - 1) as g:
                copy_xt(g + 1)
                for step in range(4):
                    pack(0, g - (NS - SUB - 1), step)
                    if step == 1:
                        guard_norms(g)
                split_units(g)
            guard_norms(NS - 1)
            split_units(NS - 1)

            dve.wait_ge(sq_done, NS)
            nc.vector.tensor_reduce(out=big[:, 0:1], in_=norm2[:], op=ALU.max, axis=AX.X).then_inc(top_done, 1)
            dve.wait_ge(top_done, 1)
            nc.vector.tensor_scalar(big[:, 0:1], big[:, 0:1], EPS_SIM, None, ALU.add).then_inc(max_done, 1)
            dve.wait_ge(scale_done, 1)
            nc.vector.tensor_scalar(big[:, 2:3], big[:, 2:3], VAL_TOP, None, ALU.mult)
            nc.vector.tensor_scalar(big[:, 3:4], big[:, 3:4], 1.0 / VAL_TOP, None, ALU.mult).then_inc(vscale_done, 1)
            dve.wait_ge(vscale_done, 1)
            with dve.Fori(0, NS) as g:
                dve.wait_ge(vh_done, g + 1)
                nc.vector.scalar_tensor_tensor(values[:, ds(g * SUB, SUB), LOW:LOW + D], Wh[:, ds(g * SUB, SUB), :],
                                               big[:, 2:3], values[:, ds(g * SUB, SUB), 0:D],
                                               ALU.mult, ALU.subtract).then_inc(vl_done, 1)

            def unpack(s, c):
                since(dve, masked, UPS * s + UNITS * c)
                w = words[:, ds(s, 1), ds(c, 1), :].rearrange("p o a w -> p (o a w)")
                for b in range(BITS):
                    last = nc.vector.tensor_scalar(mask[:, b, :], w, 14 - b, 0x4000,
                                                   ALU.logical_shift_left, ALU.bitwise_and)
                last.then_inc(unpacked, 1)
                dve.wait_ge(unpacked, NC * s + c + 1)
                own = mask16[:, ds(s, 1), ds(c * P, P)].rearrange("p o n -> p (o n)")
                nc.vector.tensor_tensor(out=own, in0=own, in1=diag2[:], op=ALU.max).then_inc(diag_done, 1)
                dve.wait_ge(diag_done, NC * s + c + 1)

            def unit_mask(s, c, q):
                n = UPS * s + UNITS * c + q
                dve.wait_ge(exps, n + 1)
                nc.vector.tensor_tensor(out=sim_ps[q % 2], in0=sim_ps[q % 2], in1=mask_pairs[:, q, :],
                                        op=ALU.mult).then_inc(masked, 1)

            def unit_low(s, c, q):
                n = UPS * s + UNITS * c + q
                dve.wait_ge(highs, n + 1)
                nc.vector.tensor_tensor(out=Pl[:, q, :, :].rearrange("p k w -> p (k w)"), in0=sim_ps[q % 2],
                                        in1=Ph[:, q, :, :].rearrange("p k w -> p (k w)"),
                                        op=ALU.subtract).then_inc(lows, 1)

            def read_attention(s):
                dve.wait_ge(attended, UPS * (s + 1))
                since(dve, attn_read, s)
                since(dve, ln_done, s)
                nc.vector.reciprocal(rsum[:], out_ps[:, :, D]).then_inc(rs_done, 1)
                dve.wait_ge(rs_done, s + 1)
                nc.vector.tensor_scalar(rsum[:], rsum[:], big[:, 3:4], None, ALU.mult).then_inc(rs_scaled, 1)
                dve.wait_ge(rs_scaled, s + 1)
                for t in range(SUB):
                    row = X[:, ds(SUB * s + t, 1), :].rearrange("p o d -> p (o d)")
                    last = nc.vector.scalar_tensor_tensor(mixed[:, t, :], out_ps[:, t, 0:D], rsum[:, t:t + 1], row,
                                                          ALU.mult, ALU.add)
                last.then_inc(attn_read, 1)

            def moments_of(tiles, at):
                since(dve, ln_done, at)
                for t in range(SUB):
                    last = nc.vector.bn_stats(stats[:, t, :], tiles(t))
                last.then_inc(st_done, 1)
                dve.wait_ge(st_done, at + 1)
                even, odd = stats[:, :, 0:3], stats[:, :, 3:6]
                nc.vector.tensor_tensor(out=mean_sum[:], in0=even[:, :, 1], in1=odd[:, :, 1], op=ALU.add)
                nc.vector.tensor_tensor(out=mean_gap[:], in0=even[:, :, 1], in1=odd[:, :, 1], op=ALU.subtract)
                nc.vector.tensor_tensor(out=squares[:], in0=even[:, :, 2], in1=odd[:, :, 2],
                                        op=ALU.add).then_inc(parts_done, 1)
                dve.wait_ge(parts_done, 2 * at + 1)
                nc.vector.tensor_scalar(mean[:], mean_sum[:], 0.5, None, ALU.mult)
                nc.vector.tensor_tensor(out=gap2[:], in0=mean_gap[:], in1=mean_gap[:], op=ALU.mult)
                nc.vector.tensor_scalar(squares[:], squares[:], 1.0 / D, EPS_LN, ALU.mult, ALU.add).then_inc(
                    parts_done, 1)
                dve.wait_ge(parts_done, 2 * at + 2)
                nc.vector.scalar_tensor_tensor(rstd[:], gap2[:], 0.25, squares[:], ALU.mult, ALU.add).then_inc(
                    var_done, 1)

            def normalise(dst, tiles, at):
                dve.wait_ge(rstd_done, at + 1)
                for t in range(SUB):
                    last = nc.vector.tensor_scalar(dst(t), tiles(t), mean[:, t:t + 1], rstd[:, t:t + 1],
                                                   ALU.subtract, ALU.mult)
                last.then_inc(ln_done, 1)

            def x_tile(s):
                return lambda t: X[:, ds(SUB * s + t, 1), :].rearrange("p o d -> p (o d)")

            def mixed_tile(t):
                return mixed[:, t, :]

            def first_iteration(s, finish, packs):
                unpack_at(s, 0)
                for q in range(UNITS):
                    unit_mask(s, 0, q)
                    if packs:
                        pack(s + 1, 0, q)
                    unit_low(s, 0, q)
                    if finish and q == 0:
                        read_attention(s - 1)
                    if finish and q == 1:
                        dve.wait_ge(attn_read, s)
                        moments_of(mixed_tile, s - 1)
                    if finish and q == 3:
                        normalise(x_tile(s - 1), mixed_tile, s - 1)

            def unpack_at(s, c):
                dve.wait_ge(words_stored, s + 1)
                unpack(s, c)

            def softmax_tile(s, finish, packs):
                first_iteration(s, finish, packs)
                with dve.Fori(1, NC) as c:
                    unpack(s, c)
                    for q in range(UNITS):
                        unit_mask(s, c, q)
                        if packs:
                            pack(s + 1, c, q)
                        unit_low(s, c, q)

            softmax_tile(0, False, True)
            with dve.Fori(1, NS - 1) as s:
                softmax_tile(s, True, True)
            softmax_tile(NS - 1, True, False)

            def unpack_late(s, c, begin):
                w = words[:, ds(s, 1), ds(c, 1), :].rearrange("p o a w -> p (o a w)")
                for b in range(BITS):
                    if not begin:
                        dve.wait_ge(mask_used, BITS * (NC * s + c - 1) + b + 1)
                    nc.vector.tensor_scalar(mask[:, b, :], w, 14 - b, 0x4000,
                                            ALU.logical_shift_left, ALU.bitwise_and).then_inc(mask_ready, 1)

            dve.wait_ge(deg_done[0], NT)
            dve.wait_ge(deg_done[1], NT)
            nc.vector.tensor_tensor(out=rdeg[:], in0=degree[:, :, 0], in1=degree[:, :, 1], op=ALU.add).then_inc(
                deg_sum, 1)
            dve.wait_ge(deg_sum, 1)
            nc.vector.tensor_scalar(rdeg[:], rdeg[:], 1.0, None, ALU.max).then_inc(deg_max, 1)
            dve.wait_ge(deg_max, 1)
            nc.vector.reciprocal(rdeg[:], rdeg[:]).then_inc(rdeg_done, 1)
            dve.wait_ge(masked, UPS * NS)
            unpack_late(0, 0, True)

            read_attention(NS - 1)
            dve.wait_ge(attn_read, NS)
            moments_of(mixed_tile, NS - 1)
            normalise(x_tile(NS - 1), mixed_tile, NS - 1)
            dve.wait_ge(ln_done, NS)
            Xc = X[:, :, :].rearrange("p (b c) d -> p c b d", c=NC)
            x1c = x1s[:, :, :].rearrange("p (b c) d -> p c b d", c=NC)
            for c in range(NC):
                nc.vector.tensor_scalar(x1c[:, c, :, 0:D], Xc[:, c, :, :], X1_SCALE, None, ALU.mult).then_inc(x1_hi, 1)
                dve.wait_ge(x1_hi, c + 1)
                nc.vector.scalar_tensor_tensor(x1c[:, c, :, LOW:LOW + D], Xc[:, c, :, :], X1_SCALE,
                                               x1c[:, c, :, 0:D], ALU.mult, ALU.subtract).then_inc(x1_split, 1)

            def keep_aggregate(s):
                dve.wait_ge(mask_used, BITS * NC * (s + 1))
                since(dve, feat_done, s)
                nc.vector.tensor_scalar(aggT[:, 1, :], ps[:, 1, :], 1.0 / (MASK_ONE * X1_SCALE), None,
                                        ALU.mult).then_inc(agg_copied, 1)

            def finish_features(s):
                dve.wait_ge(feat_done, s + 1)
                since(dve, ln_done, NS + s)
                nc.vector.tensor_tensor(out=feat, in0=ps[:, 4:8, 0:D],
                                        in1=bias[:].rearrange("p (o d) -> p o d", o=1).broadcast_to([P, SUB, D]),
                                        op=ALU.add).then_inc(feat_b, 1)
                dve.wait_ge(feat_b, s + 1)
                for t in range(SUB):
                    last = nc.vector.scalar_tensor_tensor(feat[:, t, :], ps[:, 4 + t, D:2 * D],
                                                          rdeg[:, ds(SUB * s + t, 1)], feat[:, t, :],
                                                          ALU.mult, ALU.add)
                last.then_inc(feat_sum, 1)
                dve.wait_ge(feat_sum, s + 1)
                nc.vector.scalar_tensor_tensor(feat, feat, 0.0, X[:, ds(SUB * s, SUB), :],
                                               ALU.max, ALU.add).then_inc(feat_res, 1)
                dve.wait_ge(feat_res, s + 1)
                moments_of(lambda t: feat[:, t, :], NS + s)
                since(dve, stored, 16 * s)
                normalise(lambda t: result[:, t, :], lambda t: feat[:, t, :], NS + s)

            def layer_tile(s, begin):
                if not begin:
                    unpack_late(s, 0, False)
                with dve.Fori(1, NC) as c:
                    unpack_late(s, c, False)
                if not begin:
                    finish_features(s - 1)
                keep_aggregate(s)

            layer_tile(0, True)
            with dve.Fori(1, NS) as s:
                layer_tile(s, False)
            finish_features(NS - 1)


_INS = ['x', 'adj', 'L0_gnn_W', 'L1_gnn_W_self', 'L1_gnn_b_self', 'L1_gnn_W_nb', 'L1_gnn_b_nb',
        'L1_gnn_W_comb', 'L1_gnn_b_comb']


def kernel(**inputs):
    import numpy as _np
    import concourse.bacc as _bacc
    from concourse import mybir as _mybir
    from concourse.bass_utils import run_bass_kernel_spmd as _run

    nc = _bacc.Bacc("TRN2", target_bir_lowering=False, num_devices=1)
    arrays, args = {}, []
    for name in _INS:
        a = _np.ascontiguousarray(inputs[name])
        arrays[f"in_{name}_dram"] = a
        args.append(nc.dram_tensor(f"in_{name}_dram", a.shape, _mybir.dt.from_np(a.dtype), kind="ExternalInput").ap())
    args.append(nc.dram_tensor("out_0_dram", (N, D), _mybir.dt.float32, kind="ExternalOutput").ap())
    gnn_kernel(nc, *args)
    r = _run(nc, [arrays], core_ids=[0])
    return r.results[0]["out_0_dram"]
```

```python
import concourse.bass as bass
from concourse import mybir
from contextlib import ExitStack
import math

N, D, P = 4096, 256, 128
KD = D // P
NT = N // P
SUB = 4
SW = SUB * P
NS = N // SW
BITS = 8
NC = NT // BITS
UNITS = BITS // 2
UPS = NC * UNITS
QUARTER = N // 4
VW = 2 * D + 2
LOW = D + 2
EPS_SIM = 1e-8
EPS_LN = 1e-5
SIM_SCALE = 1024.0
VAL_TOP = 8192.0
X1_SCALE = 2048.0
MASK_ONE = 2.0
EXP_BIAS = -1.0 + 13.0 * math.log(2.0)


def gnn_kernel(nc, x, adj, w0, w_self, b_self, w_nb, b_nb, w_comb, b_comb, out):
    f32, f16, bf16 = mybir.dt.float32, mybir.dt.float16, mybir.dt.bfloat16
    u16, u8, i32 = mybir.dt.uint16, mybir.dt.uint8, mybir.dt.int32
    ALU, ACT, AX = mybir.AluOpType, mybir.ActivationFunctionType, mybir.AxisListType
    ds = bass.ds

    ctx = ExitStack()
    with ctx:
        def sb(name, shape, dt):
            return ctx.enter_context(nc.sbuf_tensor(name, shape, dt))

        def sem(name):
            return ctx.enter_context(nc.semaphore(name))

        X = sb("X", [P, NT, D], f32)
        similar = sb("similar", [P, 2, KD, N], f16)
        values = sb("values", [P, NT, VW], f16)
        words = sb("words", [P, NS, NC, SW], u16)
        mask = sb("mask", [P, BITS, SW], u16)
        adj_in = sb("adj_in", [P, 2, QUARTER], i32)
        bits = sb("bits", [P, 2, QUARTER], bf16)
        pair = sb("pair", [P, 2, SW], bf16)
        exps_split = sb("exps_split", [P, 2, 2, SUB, 2, P], f16)
        mirror_in = sb("mirror_in", [P, 2, 2, SUB, 2, P], f16)
        row_words = sb("row_words", [P, SUB, SW], bf16)
        Ph = sb("Ph", [P, UNITS, 2, SW], f16)
        Pl = sb("Pl", [P, UNITS, 2, SW], f16)
        M1 = sb("M1", [P, KD, D], f32)
        M2 = sb("M2", [P, KD, D], f32)
        bias = sb("bias", [P, D], f32)
        ident32 = sb("ident32", [P, P], f32)
        ident16 = sb("ident16", [P, P], f16)
        identb = sb("identb", [P, P], bf16)
        diag2 = sb("diag2", [P, P], f16)
        sign_junk = sb("sign_junk", [P, QUARTER], u8)
        bcol = sb("bcol", [P, 2 * KD], f32)
        norm2 = sb("norm2", [P, NT], f32)
        rnorm = sb("rnorm", [P, SUB], f32)
        mixed = sb("mixed", [P, SUB, D], f32)
        minus_half = sb("minus_half", [P, SUB], f32)
        plus_half = sb("plus_half", [P, 1], f32)
        big = sb("big", [P, 4], f32)
        exp_bias = sb("exp_bias", [P, 1], f32)
        degree = sb("degree", [P, NT, 4], f32)
        rdeg = sb("rdeg", [P, NT], f32)
        rsum = sb("rsum", [P, SUB], f32)
        stats = sb("stats", [P, SUB, 6], f32)
        mean_sum, mean_gap, gap2, squares, mean = (
            sb(n, [P, SUB], f32) for n in ("mean_sum", "mean_gap", "gap2", "squares", "mean"))
        rstd = sb("rstd", [P, SUB], f32)
        stage = sb("stage", [P, SUB, D], f32)

        Wh = words[:, :, :, :].rearrange("p s c w -> p (s c w)").bitcast(f32).rearrange(
            "p (t d) -> p t d", d=D)
        wst = Ph[:, :, :, :].rearrange("p q k w -> p (q k w)").bitcast(f32).rearrange(
            "p (a d) -> p a d", d=D)
        w0_in, wself_in, wnb_in, wcomb_in = (
            wst[:, 0:2, :], wst[:, 2:4, :], wst[:, 4:6, :], mixed[:, :, :])
        wstT = Pl[:, :, :, :].rearrange("p q k w -> p (q k w)").bitcast(f32).rearrange(
            "p (a d) -> p a d", d=D)
        w0T, wselfT, wnbT = wstT[:, 0:2, :], wstT[:, 2:4, :], wstT[:, 4:6, :]
        bcomb_in = wst[:, 6, :]
        bcast = wstT[:, 6:8, :].rearrange("p a (b n) -> p (a b) n", n=P)
        mask_flat = mask[:, :, :].rearrange("p b w -> p (b w)")
        xT = mask_flat[:, 0:4 * SW].bitcast(f32).rearrange("p (t k n) -> p t k n", t=SUB, k=KD)
        unit = mask_flat[:, 4 * SW:8 * SW].bitcast(f16).rearrange("p (h t d) -> p h t d", h=2, t=SUB)
        mask16 = mask_flat.bitcast(f16).rearrange("p (b w) -> p b w", w=SW)
        mask_pairs = mask_flat.bitcast(f16).rearrange("p (q w) -> p q w", w=2 * SW)
        x1s = values
        Xc = X[:, :, :].rearrange("p (b c) d -> p c b d", c=NC)
        x1c = x1s[:, :, :].rearrange("p (b c) d -> p c b d", c=NC)
        late = similar[:, :, :, :].rearrange("p h k n -> p (h k n)").bitcast(f32)
        aggT = late[:, 0:1024].rearrange("p (k n) -> p k n", k=KD)
        x1T = late[:, 1024:2048].rearrange("p (t k n) -> p t k n", t=SUB, k=KD)
        feat = late[:, 2048:3072].rearrange("p (t d) -> p t d", d=D)
        result = late[:, 3072:4096].rearrange("p (t d) -> p t d", d=D)

        ps = ctx.enter_context(nc.psum_tensor("ps", [P, 8, 512], f32))
        ps_flat = ps[:, :, :].rearrange("p b w -> p (b w)")
        sim_ps = [ps_flat[:, 0:1024], ps_flat[:, 1024:2048]]
        word_ps = sim_ps[1].bitcast(bf16)
        out_ps = ps[:, 4:8, :]

        kept = nc.dram_tensor("kept_exps", (NS, NC, NS, P, SUB, 2, P), f16, kind="Internal").ap()

        x_first, x_rest, w_in, wc_in = sem("x_first"), sem("x_rest"), sem("w_in"), sem("wc_in")
        w0_ready = sem("w0_ready")
        consts, staged, ln_done = sem("consts"), sem("staged"), sem("layernorm_done")
        pool_step = sem("pool_step")
        w_t, w_tc = sem("w_transposed"), sem("w_copied")
        bc_done, fused, fused_copied = sem("bias_columns"), sem("weights_fused"), sem("fused_copied")
        xt_done, xt_copied = sem("x_transposed"), sem("x_copied")
        wh_done, wh_copied, sq_done = sem("wh_done"), sem("wh_copied"), sem("squares_done")
        n2_done, rn_done = sem("norm2_done"), sem("rnorm_done")
        unit_hi, unit_done = sem("unit_high"), sem("unit_done")
        ut_done, ut_copied = sem("unit_transposed"), sem("unit_copied")
        top_done, max_done, all_max, scale_done, vscale_done = (
            sem("row_max_done"), sem("max_done"), sem("all_max"), sem("scale_done"), sem("vscale_done"))
        vh_done, vl_done = sem("values_high"), sem("values_low")
        adj_ready = [sem("adj_ready0"), sem("adj_ready1")]
        bits_done, deg_done = sem("bits_done"), sem("deg_done")
        pairs_done, sums_done = sem("pairs_done"), sem("sums_done")
        kept_done = {b: sem(f"kept_done{b}") for b in range(1, NS)}
        mirror_ready = {b: sem(f"mirror_ready{b}") for b in range(NS - 1)}
        words_t, words_stored = sem("words_transposed"), sem("words_stored")
        unpacked, diag_done = sem("unpacked"), sem("diag_done")
        sims, exps, highs, lows, masked, attended = (
            sem("sims"), sem("exps"), sem("highs"), sem("lows"), sem("masked"), sem("attended"))
        rs_done, rs_scaled, attn_read = sem("rsum_done"), sem("rsum_scaled"), sem("attn_read")
        st_done, parts_done, var_done, rstd_done = (
            sem("stats_done"), sem("moment_parts"), sem("variance_done"), sem("rstd_done"))
        deg_sum, deg_max, rdeg_done = sem("deg_sum"), sem("deg_max"), sem("rdeg_done")
        x1_hi, x1_split = sem("x1_high"), sem("x1_split")
        mask_ready, mask_used = sem("mask_ready"), sem("mask_used")
        agg_copied = sem("agg_copied")
        x1t_done, x1t_copied = sem("x1_transposed"), sem("x1t_copied")
        feat_done, feat_b, feat_sum, feat_res = (
            sem("features_done"), sem("features_biased"), sem("features_summed"), sem("features_residual"))
        stored = sem("stored")

        block = ctx.enter_context(nc.Block())

        def since(eng, s, v):
            if not (isinstance(v, int) and v <= 0):
                eng.wait_ge(s, v)

        def pair_of(k):
            return UNITS - 1 - k % UNITS

        def computed(s, k):
            return [kk for kk in range(2) if 2 * pair_of(k) + kk >= s]

        def mirrored(s, k):
            return [kk for kk in range(2) if 2 * pair_of(k) + kk < s]

        def kept_blocks(s, k):
            return [2 * pair_of(k) + kk for kk in computed(s, k) if 2 * pair_of(k) + kk > s]

        def last_in_buffer(s, c, k):
            if k >= 2:
                return s, c, k - 2
            if isinstance(c, int) and c == 0:
                s, c = s - 1, NC
            if s < 0:
                return None
            return s, c - 1, max(i for i in (k, k + 2) if computed(s, i))

        def units_computed(s):
            return sum(1 for k in range(UNITS) if computed(s, k))

        def computed_before(s, c, k):
            return NC * sum(units_computed(i) for i in range(s)) + units_computed(s) * c + k

        VALUE_ORDER = [0] + list(range(NS - 1, 0, -1))

        def value_groups(k):
            return [(at, g) for at, g in enumerate(VALUE_ORDER)
                    if (g // 2 == pair_of(k) if g else k == 0)]

        def values_split(k):
            return sum(len(value_groups(i)) for i in range(k + 1))

        def unit_at(s, c, k):
            return UPS * s + UNITS * c + k

        def quarter(tile, r):
            return 4 * tile + r + 1

        @block.sync
        def _(sp):
            xv = x.rearrange("(t p) d -> p t d", p=P)
            sp.dma_start(stage[:, :, :], xv[:, 0:SUB, :]).then_inc(staged, 16)
            sp.dma_start(X[:, 0:2 * SUB, :], xv[:, 0:2 * SUB, :]).then_inc(x_first, 16)
            def load_adj(tile, r):
                sp.dma_start(adj_in[:, r % 2, :],
                             adj[ds(tile * P, P), r * QUARTER:(r + 1) * QUARTER]).then_inc(adj_ready[r % 2], 16)

            def next_adj(tile, r):
                sp.wait_ge(bits_done, quarter(tile, r))
                load_adj(tile if r < 2 else tile + 1, (r + 2) % 4)

            def stage_x(g):
                since(sp, xt_done, g)
                sp.dma_start(stage[:, :, :], X[:, ds(g * SUB, SUB), :]).then_inc(staged, 16)

            sp.wait_ge(x_first, 16)
            stage_x(1)
            sp.dma_start(X[:, 2 * SUB:NT, :], xv[:, 2 * SUB:NT, :]).then_inc(x_rest, 16)
            load_adj(0, 0)
            load_adj(0, 1)
            sp.wait_ge(x_rest, 16)
            with sp.Fori(2, NS - SUB + 1) as g:
                stage_x(g)
            with sp.Fori(0, SUB - 1) as t:
                stage_x(t + (NS - SUB + 1))
                for r in range(4):
                    next_adj(t, r)
            for r in range(4):
                next_adj(SUB - 1, r)

            def load_mirror(s, c, k):
                for kk in mirrored(s, k):
                    b = 2 * pair_of(k) + kk
                    since(sp, sims, unit_at(s, c, k) - 1)
                    sp.wait_ge(kept_done[s], 16 * NC * s)
                    sp.dma_start(mirror_in[:, k % 2, kk, :, :, :],
                                 kept[b, ds(c, 1), s, :, :, :, :].rearrange("o p t h n -> (o p) t h n")).then_inc(
                                     mirror_ready[b], 16)

            def keep_exps(s, c, k):
                for kk in computed(s, k):
                    b = 2 * pair_of(k) + kk
                    if b > s:
                        sp.wait_ge(lows, computed_before(s, c, k) + 1)
                        sp.dma_start(kept[s, :, b, :, ds(c, 1), :, :].rearrange("t p o h n -> p t (o h n)"),
                                     exps_split[:, k % 2, kk, :, :, :].rearrange("p t h n -> p t (h n)")).then_inc(
                                         kept_done[b], 16)

            def traffic(s, c):
                end = isinstance(c, int) and c == NC - 1
                for k in range(UNITS):
                    if k + 2 < UNITS:
                        load_mirror(s, c, k + 2)
                    elif not end:
                        load_mirror(s, c + 1, k - 2)
                    elif s + 1 < NS:
                        load_mirror(s + 1, 0, k - 2)
                    if s + 1 < NS and not (s + 2 == NS and end and k >= 2):
                        next_adj(SUB * (s + 1) + c, k)
                    keep_exps(s, c, k)

            for s in range(NS):
                with sp.Fori(0, NC - 1) as c:
                    traffic(s, c)
                traffic(s, NC - 1)

            def stage_x1(s):
                sp.dma_start(stage[:, :, :], X[:, ds(s * SUB, SUB), :]).then_inc(staged, 16)

            def store(s):
                sp.wait_ge(ln_done, NS + s + 1)
                sp.dma_start(out[ds(s * SW, SW), :].rearrange("(t p) d -> p t d", p=P),
                             result).then_inc(stored, 16)

            sp.wait_ge(ln_done, NS)
            stage_x1(0)
            with sp.Fori(1, NS) as s:
                sp.wait_ge(x1t_done, s)
                stage_x1(s)
                store(s - 1)
            store(NS - 1)
            sp.wait_ge(stored, 16 * NS)

        @block.gpsimd
        def _(pool):
            for t in (ident32, ident16, identb, diag2):
                nc.gpsimd.memset(t[:], 0.0)
            nc.gpsimd.memset(minus_half[:], -0.5)
            nc.gpsimd.memset(plus_half[:], 0.5)
            nc.gpsimd.memset(exp_bias[:], EXP_BIAS).then_inc(pool_step, 1)
            pool.wait_ge(pool_step, 1)
            for t, one in ((ident32, 1.0), (ident16, 1.0), (identb, 1.0), (diag2, MASK_ONE)):
                last = nc.gpsimd.affine_select(out=t[:], in_=t[:], compare_op=ALU.not_equal, fill=one, base=0,
                                               pattern=[[-1, P]], channel_multiplier=1)
            last.then_inc(consts, 1)

            with pool.Fori(0, NS) as g:
                pool.wait_ge(n2_done, g + 1)
                nc.gpsimd.tensor_tensor(out=rnorm[:], in0=rnorm[:], in1=minus_half[:], op=ALU.pow).then_inc(rn_done, 1)
            pool.wait_ge(max_done, 1)
            nc.gpsimd.partition_all_reduce(big[:, 1:2], big[:, 0:1], P, bass.bass_isa.ReduceOp.max).then_inc(all_max, 1)
            pool.wait_ge(all_max, 1)
            nc.gpsimd.tensor_tensor(out=big[:, 2:3], in0=big[:, 1:2], in1=minus_half[:, 0:1], op=ALU.pow)
            nc.gpsimd.tensor_tensor(out=big[:, 3:4], in0=big[:, 1:2], in1=plus_half[:], op=ALU.pow).then_inc(
                scale_done, 1)
            with pool.Fori(0, 2 * NS) as at:
                pool.wait_ge(var_done, at + 1)
                nc.gpsimd.tensor_tensor(out=rstd[:], in0=rstd[:], in1=minus_half[:], op=ALU.pow).then_inc(
                    rstd_done, 1)

        @block.tensor
        def _(pe):
            def transpose_weights(bank, w):
                for ko in range(KD):
                    for ki in range(KD):
                        last = nc.tensor.transpose(ps[:, bank, ki * D + ko * P:ki * D + (ko + 1) * P],
                                                   w[:, ko, ki * P:(ki + 1) * P], ident32[:])
                last.then_inc(w_t, 1)

            pe.wait_ge(consts, 1)
            pe.wait_ge(w0_ready, 16)
            transpose_weights(4, w0_in)

            def transpose_x(g):
                since(pe, xt_copied, g)
                pe.wait_ge(staged, 16 * g + 16)
                for t in range(SUB):
                    for k in range(KD):
                        at = (t * KD + k) * P
                        last = nc.tensor.transpose(ps_flat[:, at:at + P],
                                                   stage[:, t, k * P:(k + 1) * P], ident32[:])
                last.then_inc(xt_done, 1)

            def project(g):
                pe.wait_ge(xt_copied, g + 1)
                pe.wait_ge(w_tc, 1)
                since(pe, wh_copied, g)
                for t in range(SUB):
                    for k in range(KD):
                        last = nc.tensor.matmul(ps_flat[:, 1024 + t * D:1024 + (t + 1) * D], xT[:, t, k, :],
                                                w0T[:, k, :], start=(k == 0), stop=(k == KD - 1))
                last.then_inc(wh_done, 1)

            def transpose_unit(g):
                pe.wait_ge(unit_done, g + 1)
                since(pe, ut_copied, g)
                dst = ps_flat[:, 3072:4096].bitcast(f16)
                for h in range(2):
                    for k in range(KD):
                        for t in range(SUB):
                            at = (h * KD + k) * SW + t * P
                            last = nc.tensor.transpose(dst[:, at:at + P], unit[:, h, t, k * P:(k + 1) * P],
                                                       ident16[:])
                last.then_inc(ut_done, 1)

            transpose_x(0)
            transpose_x(1)
            project(0)
            with pe.Fori(1, NS - 1) as g:
                transpose_x(g + 1)
                project(g)
                transpose_unit(g - 1)
            project(NS - 1)
            transpose_unit(NS - 2)
            pe.wait_ge(w_in, 16 * 2)
            pe.wait_ge(w_tc, 1)
            transpose_weights(4, wself_in)
            transpose_weights(5, wnb_in)
            pe.wait_ge(wh_copied, NS)
            pe.wait_ge(w_tc, 3)
            pe.wait_ge(wc_in, 16 * 6)
            pe.wait_ge(bc_done, 1)
            for i, wT in enumerate((wselfT, wnbT)):
                for kd in range(KD):
                    for km in range(KD):
                        nc.tensor.matmul(ps[:, 4 + i, kd * D:(kd + 1) * D], wT[:, km, kd * P:(kd + 1) * P],
                                         wcomb_in[:, KD * i + km, :], start=(km == 0), stop=(km == KD - 1))
            for k in range(2 * KD):
                last = nc.tensor.matmul(ps[:, 3, 0:D], bcast[:, k, :], wcomb_in[:, k, :],
                                        start=(k == 0), stop=(k == 2 * KD - 1))
            last.then_inc(fused, 1)

            transpose_unit(NS - 1)

            def similarities(s, c, k):
                n = unit_at(s, c, k)
                since(pe, masked, n - 1)
                for kk in mirrored(s, k):
                    b = 2 * pair_of(k) + kk
                    pe.wait_ge(mirror_ready[b], 16 * (NC * (s - b - 1) + c + 1))
                    dst = sim_ps[k % 2][:, kk * SW:(kk + 1) * SW].bitcast(f16)
                    for h in range(2):
                        for t in range(SUB):
                            at = h * SW + t * P
                            last = nc.tensor.transpose(dst[:, at:at + P], mirror_in[:, k % 2, kk, t, h, :], ident16[:])
                for kk in computed(s, k):
                    jb = NC * (2 * pair_of(k) + kk) + c
                    terms = [(hj, hi, d) for hj, hi in ((0, 0), (0, 1), (1, 0)) for d in range(KD)]
                    for i, (hj, hi, d) in enumerate(terms):
                        last = nc.tensor.matmul(sim_ps[k % 2][:, kk * SW:(kk + 1) * SW],
                                                similar[:, hj, d, ds(jb * P, P)],
                                                similar[:, hi, d, s * SW:(s + 1) * SW],
                                                start=(i == 0), stop=(i == len(terms) - 1))
                last.then_inc(sims, 1)

            def attend(s, c, k):
                n = unit_at(s, c, k)
                first = isinstance(c, int) and c == 0 and k == 0
                end = isinstance(c, int) and c == NC - 1 and k == UNITS - 1
                pe.wait_ge(masked, n + 1)
                if s == 0 and isinstance(c, int) and c == 0:
                    pe.wait_ge(vl_done, values_split(k))
                if first:
                    since(pe, attn_read, s)
                for kk in range(2):
                    jb = NC * (2 * pair_of(k) + kk) + c
                    row = values[:, ds(jb, 1), :].rearrange("p o w -> p (o w)")
                    for t in range(SUB):
                        hi = Ph[:, k, kk, t * P:(t + 1) * P]
                        lo = Pl[:, k, kk, t * P:(t + 1) * P]
                        nc.tensor.matmul(out_ps[:, t, 0:D + 1], hi, row[:, 0:D + 1],
                                         start=first and kk == 0, stop=False, skip_group_check=True)
                        nc.tensor.matmul(out_ps[:, t, 0:D], hi, row[:, LOW:LOW + D],
                                         start=False, stop=False, skip_group_check=True)
                        last = nc.tensor.matmul(out_ps[:, t, 0:D + 1], lo, row[:, 0:D + 1],
                                                start=False, stop=end and kk == 1, skip_group_check=True)
                last.then_inc(attended, 1)

            def transpose_words(s):
                pe.wait_ge(sums_done, 3 * SUB * (s + 1))
                since(pe, masked, UPS * s)
                for t in range(SUB):
                    for c in range(NC):
                        last = nc.tensor.transpose(word_ps[:, c * SW + t * P:c * SW + (t + 1) * P],
                                                   row_words[:, t, c * P:(c + 1) * P], identb[:])
                last.then_inc(words_t, 1)

            def attention_tile(s, begin):
                if begin:
                    pe.wait_ge(ut_copied, NS)
                else:
                    attend(s - 1, NC - 1, UNITS - 2)
                similarities(s, 0, 0)
                if begin:
                    pe.wait_ge(fused_copied, 2)
                transpose_words(s)
                if not begin:
                    attend(s - 1, NC - 1, UNITS - 1)
                pe.wait_ge(words_stored, 2 * s + 2)
                similarities(s, 0, 1)
                for q in range(2, UNITS):
                    similarities(s, 0, q)
                    attend(s, 0, q - 2)
                with pe.Fori(1, NC) as c:
                    for q in range(UNITS):
                        similarities(s, c, q)
                        attend(s, c - 1 if q < 2 else c, (q - 2) % UNITS)

            for s in range(NS):
                attention_tile(s, s == 0)
            for k in (UNITS - 2, UNITS - 1):
                attend(NS - 1, NC - 1, k)

            def aggregate(s, c, begin):
                first = isinstance(c, int) and c == 0
                end = isinstance(c, int) and c == NC - 1
                if begin:
                    pe.wait_ge(x1_split, 1 if first else c + 2)
                for b in range(BITS):
                    pe.wait_ge(mask_ready, BITS * (NC * s + c) + b + 1)
                    if begin and first and b == BITS - 1:
                        pe.wait_ge(x1_split, 2)
                    for k in range(KD):
                        for h in range(2):
                            jb = NC * b + c
                            at = (LOW if h else 0) + k * P
                            last = nc.tensor.matmul(ps[:, k, :],
                                                    x1s[:, ds(jb, 1), at:at + P].rearrange("p o n -> p (o n)"),
                                                    mask16[:, b, :],
                                                    start=first and b == 0 and h == 0,
                                                    stop=end and b == BITS - 1 and h == 1, skip_group_check=True)
                    last.then_inc(mask_used, 1)

            def transpose_x1(s):
                since(pe, x1t_copied, s)
                pe.wait_ge(staged, 16 * (NS + s + 1))
                for t in range(SUB):
                    for k in range(KD):
                        at = 1024 + (t * KD + k) * P
                        last = nc.tensor.transpose(
                            ps_flat[:, at:at + P],
                            stage[:, t, k * P:(k + 1) * P], ident32[:])
                last.then_inc(x1t_done, 1)

            def features(s):
                pe.wait_ge(x1t_copied, s + 1)
                pe.wait_ge(agg_copied, 2 * s + 2)
                since(pe, feat_sum, s)
                for t in range(SUB):
                    for k in range(KD):
                        nc.tensor.matmul(ps[:, 4 + t, 0:D], x1T[:, t, k, :], M1[:, k, :],
                                         start=(k == 0), stop=(k == KD - 1))
                    for k in range(KD):
                        last = nc.tensor.matmul(ps[:, 4 + t, D:2 * D], aggT[:, k, t * P:(t + 1) * P], M2[:, k, :],
                                                start=(k == 0), stop=(k == KD - 1))
                last.then_inc(feat_done, 1)

            def layer_tile(s, begin):
                if not begin:
                    pe.wait_ge(agg_copied, 2 * s)
                aggregate(s, 0, begin)
                if not begin:
                    features(s - 1)
                with pe.Fori(1, NC - 1) as c:
                    aggregate(s, c, begin)
                aggregate(s, NC - 1, begin)
                transpose_x1(s)

            layer_tile(0, True)
            with pe.Fori(1, NS) as s:
                layer_tile(s, False)
            features(NS - 1)

        @block.scalar
        def _(act):
            def rows(w):
                return w.rearrange("(k p) d -> p k d", p=P)
            act.dma_start(w0_in, rows(w0)).then_inc(w0_ready, 16)
            for dst, w in ((wself_in, w_self), (wnb_in, w_nb)):
                act.dma_start(dst, rows(w)).then_inc(w_in, 16)
            act.dma_start(wcomb_in, rows(w_comb)).then_inc(wc_in, 16)
            for i, b in enumerate((b_self, b_nb)):
                for k in range(KD):
                    act.dma_start(bcol[:, KD * i + k:KD * i + k + 1],
                                  b[k * P:(k + 1) * P].rearrange("(p o) -> p o", o=1)).then_inc(wc_in, 16)
            act.dma_start(bcomb_in, b_comb.rearrange("(o d) -> o d", o=1).broadcast_to([P, D])).then_inc(wc_in, 16)


            def keep_wh(g):
                act.wait_ge(wh_done, g + 1)
                wh = Wh[:, ds(g * SUB, SUB), :]
                nc.scalar.copy(wh, ps_flat[:, 1024:2048].rearrange("p (t d) -> p t d", d=D)).then_inc(wh_copied, 1)
                act.wait_ge(wh_copied, g + 1)
                for t in range(SUB):
                    last = nc.scalar.activation(sign_junk[:, t * D:(t + 1) * D],
                                                Wh[:, ds(g * SUB + t, 1), :].rearrange("p o d -> p (o d)"),
                                                ACT.Square, accum_out=norm2[:, ds(g * SUB + t, 1)])
                last.then_inc(sq_done, 1)

            def keep_unit(g):
                act.wait_ge(ut_done, g + 1)
                nc.scalar.copy(similar[:, :, :, ds(g * SW, SW)].rearrange("p h k n -> p (h k) n"),
                               ps_flat[:, 3072:4096].bitcast(f16).rearrange("p (a n) -> p a n", a=2 * KD)).then_inc(
                                   ut_copied, 1)

            def count_degree(tile, r, squared=None):
                act.wait_ge(bits_done, quarter(tile, r))
                act.wait_ge(sq_done, NS if squared is None else squared)
                since(act, deg_done, quarter(tile, r) - 1)
                nc.scalar.activation(sign_junk[:], bits[:, r % 2, :], ACT.Sign,
                                     accum_out=degree[:, ds(tile, 1), r:r + 1].rearrange("p o h -> p (o h)")
                                     ).then_inc(deg_done, 1)

            keep_wh(0)
            with act.Fori(1, NS - SUB - 1) as g:
                keep_wh(g)
                keep_unit(g - 1)
            with act.Fori(NS - SUB - 1, NS - 2) as g:
                keep_wh(g)
                keep_unit(g - 1)
                for r in range(4):
                    count_degree(g - (NS - SUB - 1), r, g + 1)
            keep_wh(NS - 2)
            keep_unit(NS - 3)
            for r in range(3):
                count_degree(SUB - 1, r, NS - 1)
            keep_wh(NS - 1)
            keep_unit(NS - 2)
            for i, wT in enumerate((wselfT, wnbT)):
                act.wait_ge(w_t, 2 + i)
                nc.scalar.copy(wT, ps[:, 4 + i, :].rearrange("p (k d) -> p k d", k=KD)).then_inc(w_tc, 1)
            act.wait_ge(fused, 1)
            nc.scalar.copy(M1[:, :, :], ps[:, 4, :].rearrange("p (k d) -> p k d", k=KD))
            nc.scalar.copy(M2[:, :, :], ps[:, 5, :].rearrange("p (k d) -> p k d", k=KD)).then_inc(fused_copied, 1)
            keep_unit(NS - 1)
            def high_values(k):
                for _, g in value_groups(k):
                    nc.scalar.activation(values[:, g * SUB:(g + 1) * SUB, 0:D], Wh[:, g * SUB:(g + 1) * SUB, :],
                                         ACT.Copy, scale=big[:, 2:3]).then_inc(vh_done, 1)

            act.wait_ge(vscale_done, 1)
            high_values(0)

            def unit_exps(s, c, k):
                kks = computed(s, k)
                if not kks:
                    return
                f = computed_before(s, c, k)
                z = sim_ps[k % 2][:, kks[0] * SW:2 * SW]
                act.wait_ge(sims, unit_at(s, c, k) + 1)
                nc.scalar.activation(z, z, ACT.Exp, bias=exp_bias[:], scale=1.0 / SIM_SCALE ** 2).then_inc(exps, 1)
                act.wait_ge(exps, f + 1)
                since(act, masked, unit_at(s, c, k) - 1)
                before = last_in_buffer(s, c, k)
                if before:
                    s0, c0, k0 = before
                    for b in kept_blocks(s0, k0):
                        act.wait_ge(kept_done[b], 16 * (NC * s0 + c0 + 1))
                nc.scalar.copy(exps_split[:, k % 2, kks[0]:2, :, 0, :].rearrange("p k t n -> p (k t) n"),
                               z.rearrange("p (t n) -> p t n", n=P)).then_inc(highs, 1)

            def iteration(s, c, begin):
                for k in range(UNITS):
                    if begin and k == 0:
                        act.wait_ge(words_t, s + 1)
                        act.wait_ge(vl_done, NS if s else 1)
                        nc.scalar.copy(words[:, s, 0, :], word_ps[:, 0:SW]).then_inc(words_stored, 1)
                    unit_exps(s, c, k)
                    if begin and k == 0:
                        nc.scalar.copy(words[:, s, 1:NC, :].rearrange("p c w -> p (c w)"),
                                       word_ps[:, SW:NC * SW]).then_inc(words_stored, 1)
                    if begin and s == 0 and k + 1 < UNITS:
                        high_values(k + 1)
                    tile = SUB * (s + 1) + c
                    if s + 1 < NS or (begin and k == 0):
                        count_degree(tile if k else tile - 1, (k - 1) % 4)

            for s in range(NS):
                iteration(s, 0, True)
                with act.Fori(1, NC) as c:
                    iteration(s, c, False)

            def high_x1(c, b0, b1):
                nc.scalar.mul(x1c[:, c, b0:b1, 0:D], Xc[:, c, b0:b1, :], X1_SCALE).then_inc(x1_hi, 1)

            act.wait_ge(attended, UPS * NS)
            act.wait_ge(ln_done, NS - 1)
            high_x1(0, 0, BITS - 1)
            act.wait_ge(ln_done, NS)
            high_x1(0, BITS - 1, BITS)
            for c in range(1, NC):
                high_x1(c, 0, BITS)

            with act.Fori(0, NS) as s:
                act.wait_ge(mask_used, BITS * NC * (s + 1))
                since(act, feat_done, s)
                nc.scalar.mul(aggT[:, 0, :], ps[:, 0, :], 1.0 / (MASK_ONE * X1_SCALE)).then_inc(agg_copied, 1)
                act.wait_ge(x1t_done, s + 1)
                nc.scalar.copy(x1T, ps_flat[:, 1024:2048].rearrange("p (t k n) -> p t k n", t=SUB, k=KD)).then_inc(
                    x1t_copied, 1)

        @block.vector
        def _(dve):
            dve.wait_ge(w_t, 1)
            nc.vector.tensor_copy(w0T, ps[:, 4, :].rearrange("p (k d) -> p k d", k=KD)).then_inc(w_tc, 1)
            nc.vector.memset(values[:, :, D:D + 2], 1.0)

            def copy_xt(g):
                dve.wait_ge(xt_done, g + 1)
                since(dve, wh_done, g)
                nc.vector.tensor_copy(xT, ps_flat[:, 0:1024].rearrange("p (t k n) -> p t k n", t=SUB, k=KD)).then_inc(
                    xt_copied, 1)

            def guard_norms(g):
                dve.wait_ge(sq_done, g + 1)
                since(dve, unit_done, g)
                nc.vector.tensor_scalar(rnorm[:], norm2[:, ds(g * SUB, SUB)], EPS_SIM, 1.0 / SIM_SCALE ** 2,
                                        ALU.add, ALU.mult).then_inc(n2_done, 1)

            def split_units(g):
                dve.wait_ge(rn_done, g + 1)
                since(dve, ut_done, g)
                for t in range(SUB):
                    row = Wh[:, ds(g * SUB + t, 1), :].rearrange("p o d -> p (o d)")
                    last = nc.vector.tensor_scalar(unit[:, 0, t, :], row, rnorm[:, t:t + 1], None, ALU.mult)
                last.then_inc(unit_hi, 1)
                dve.wait_ge(unit_hi, g + 1)
                for t in range(SUB):
                    row = Wh[:, ds(g * SUB + t, 1), :].rearrange("p o d -> p (o d)")
                    last = nc.vector.scalar_tensor_tensor(unit[:, 1, t, :], row, rnorm[:, t:t + 1],
                                                          unit[:, 0, t, :], ALU.mult, ALU.subtract)
                last.then_inc(unit_done, 1)

            def pack(tile, r):
                m = quarter(tile, r)
                dve.wait_ge(adj_ready[r % 2], 16 * (2 * tile + r // 2) + 16)
                since(dve, deg_done, m - 2)
                since(dve, pairs_done, m - 2)
                for i in range(2):
                    last = nc.vector.tensor_scalar(bits[:, r % 2, i * SW:(i + 1) * SW],
                                                   adj_in[:, r % 2, i * SW:(i + 1) * SW],
                                                   0, float(2 ** (2 * r + i)), ALU.is_gt, ALU.mult)
                last.then_inc(bits_done, 1)
                dve.wait_ge(bits_done, m)
                since(dve, sums_done, 3 * tile + r - 1)
                nc.vector.tensor_tensor(out=pair[:, r % 2, :], in0=bits[:, r % 2, 0:SW],
                                        in1=bits[:, r % 2, SW:2 * SW], op=ALU.add).then_inc(pairs_done, 1)
                dve.wait_ge(pairs_done, m)

            def add_pair(s, t, r):
                tile = SUB * s + t
                if r == 0:
                    return
                if r == 1:
                    since(dve, words_t, s)
                row = row_words[:, ds(t, 1), :].rearrange("p o w -> p (o w)")
                if r > 1:
                    dve.wait_ge(sums_done, 3 * tile + r - 1)
                nc.vector.tensor_tensor(out=row, in0=pair[:, 0, :] if r == 1 else row, in1=pair[:, r % 2, :],
                                        op=ALU.add).then_inc(sums_done, 1)

            copy_xt(0)
            dve.wait_ge(wc_in, 16 * 6)
            dve.wait_ge(consts, 1)
            for k in range(2 * KD):
                last = nc.vector.tensor_scalar(bcast[:, k, :], ident32[:], 0.0, bcol[:, k:k + 1], ALU.mult, ALU.add)
            last.then_inc(bc_done, 1)
            with dve.Fori(0, NS - SUB - 1) as g:
                copy_xt(g + 1)
                guard_norms(g)
                split_units(g)

            def group_and_words(g):
                copy_xt(g + 1)
                for r in range(4):
                    pack(g - (NS - SUB - 1), r)
                    add_pair(0, g - (NS - SUB - 1), r)
                    if r == 1:
                        guard_norms(g)
                split_units(g)

            group_and_words(NS - SUB - 1)
            with dve.Fori(NS - SUB, NS - 1) as g:
                group_and_words(g)
            guard_norms(NS - 1)
            dve.wait_ge(sq_done, NS)
            nc.vector.tensor_reduce(out=big[:, 0:1], in_=norm2[:], op=ALU.max, axis=AX.X).then_inc(top_done, 1)
            dve.wait_ge(top_done, 1)
            nc.vector.tensor_scalar(big[:, 0:1], big[:, 0:1], EPS_SIM, None, ALU.add).then_inc(max_done, 1)
            split_units(NS - 1)
            dve.wait_ge(fused, 1)
            nc.vector.tensor_tensor(out=bias[:], in0=ps[:, 3, 0:D], in1=bcomb_in, op=ALU.add).then_inc(
                fused_copied, 1)

            dve.wait_ge(scale_done, 1)
            nc.vector.tensor_scalar(big[:, 2:3], big[:, 2:3], VAL_TOP, None, ALU.mult)
            nc.vector.tensor_scalar(big[:, 3:4], big[:, 3:4], 1.0 / VAL_TOP, None, ALU.mult).then_inc(vscale_done, 1)
            dve.wait_ge(vscale_done, 1)

            def low_values(k):
                for at, g in value_groups(k):
                    dve.wait_ge(vh_done, at + 1)
                    nc.vector.scalar_tensor_tensor(values[:, g * SUB:(g + 1) * SUB, LOW:LOW + D],
                                                   Wh[:, g * SUB:(g + 1) * SUB, :], big[:, 2:3],
                                                   values[:, g * SUB:(g + 1) * SUB, 0:D],
                                                   ALU.mult, ALU.subtract).then_inc(vl_done, 1)

            low_values(0)

            def unpack(s, c, k):
                n = unit_at(s, c, k)
                since(dve, masked, n - (UNITS - 1))
                w = words[:, s, ds(c, 1), :].rearrange("p a w -> p (a w)")
                for b in (2 * pair_of(k), 2 * pair_of(k) + 1):
                    last = nc.vector.tensor_scalar(mask[:, b, :], w, 14 - b, 0x4000,
                                                   ALU.logical_shift_left, ALU.bitwise_and)
                last.then_inc(unpacked, 1)
                if s // 2 == pair_of(k):
                    dve.wait_ge(unpacked, n + 1)
                    own = mask16[:, s, ds(c * P, P)]
                    nc.vector.tensor_tensor(out=own, in0=own, in1=diag2[:], op=ALU.max).then_inc(diag_done, 1)

            def unit_low(s, c, k):
                kks = computed(s, k)
                if not kks:
                    return
                dve.wait_ge(highs, computed_before(s, c, k) + 1)
                split = exps_split[:, k % 2, kks[0]:2, :, :, :].rearrange("p k t h n -> p (k t) h n")
                z = sim_ps[k % 2][:, kks[0] * SW:2 * SW].rearrange("p (t n) -> p t n", n=P)
                nc.vector.tensor_tensor(out=split[:, :, 1, :], in0=z, in1=split[:, :, 0, :],
                                        op=ALU.subtract).then_inc(lows, 1)

            def unit_mask(s, c, k):
                n = unit_at(s, c, k)
                dve.wait_ge(unpacked, n + 1)
                if s // 2 == pair_of(k):
                    dve.wait_ge(diag_done, NC * s + c + 1)
                since(dve, attended, n - (UNITS - 1))
                if mirrored(s, k):
                    dve.wait_ge(sims, n + 1)
                for kk in mirrored(s, k):
                    exps_t = sim_ps[k % 2][:, kk * SW:(kk + 1) * SW].bitcast(f16)
                    for h, dst in enumerate((Ph, Pl)):
                        last = nc.vector.tensor_tensor(out=dst[:, k, kk, :], in0=exps_t[:, h * SW:(h + 1) * SW],
                                                       in1=mask16[:, 2 * pair_of(k) + kk, :], op=ALU.mult)
                kks = computed(s, k)
                if kks:
                    dve.wait_ge(lows, computed_before(s, c, k) + 1)
                    b = 2 * pair_of(k)
                    m = mask16[:, b + kks[0]:b + 2, :].rearrange("p k (t n) -> p (k t) n", n=P)
                    split = exps_split[:, k % 2, kks[0]:2, :, :, :].rearrange("p k t h n -> p (k t) h n")
                    for h, dst in enumerate((Ph, Pl)):
                        last = nc.vector.tensor_tensor(
                            out=dst[:, k, kks[0]:2, :].rearrange("p k (t n) -> p (k t) n", n=P),
                            in0=split[:, :, h, :], in1=m, op=ALU.mult)
                last.then_inc(masked, 1)

            def read_attention(s):
                dve.wait_ge(attended, UPS * (s + 1))
                since(dve, attn_read, s)
                since(dve, ln_done, s)
                nc.vector.reciprocal(rsum[:], out_ps[:, :, D]).then_inc(rs_done, 1)
                dve.wait_ge(rs_done, s + 1)
                nc.vector.tensor_scalar(rsum[:], rsum[:], big[:, 3:4], None, ALU.mult).then_inc(rs_scaled, 1)
                dve.wait_ge(rs_scaled, s + 1)
                for t in range(SUB):
                    row = X[:, ds(SUB * s + t, 1), :].rearrange("p o d -> p (o d)")
                    last = nc.vector.scalar_tensor_tensor(mixed[:, t, :], out_ps[:, t, 0:D], rsum[:, t:t + 1], row,
                                                          ALU.mult, ALU.add)
                last.then_inc(attn_read, 1)

            def moments_of(tiles, at):
                since(dve, ln_done, at)
                for t in range(SUB):
                    last = nc.vector.bn_stats(stats[:, t, :], tiles(t))
                last.then_inc(st_done, 1)
                dve.wait_ge(st_done, at + 1)
                even, odd = stats[:, :, 0:3], stats[:, :, 3:6]
                nc.vector.tensor_tensor(out=mean_sum[:], in0=even[:, :, 1], in1=odd[:, :, 1], op=ALU.add)
                nc.vector.tensor_tensor(out=mean_gap[:], in0=even[:, :, 1], in1=odd[:, :, 1], op=ALU.subtract)
                nc.vector.tensor_tensor(out=squares[:], in0=even[:, :, 2], in1=odd[:, :, 2],
                                        op=ALU.add).then_inc(parts_done, 1)
                dve.wait_ge(parts_done, 2 * at + 1)
                nc.vector.tensor_scalar(mean[:], mean_sum[:], 0.5, None, ALU.mult)
                nc.vector.tensor_tensor(out=gap2[:], in0=mean_gap[:], in1=mean_gap[:], op=ALU.mult)
                nc.vector.tensor_scalar(squares[:], squares[:], 1.0 / D, EPS_LN, ALU.mult, ALU.add).then_inc(
                    parts_done, 1)
                dve.wait_ge(parts_done, 2 * at + 2)
                nc.vector.scalar_tensor_tensor(rstd[:], gap2[:], 0.25, squares[:], ALU.mult, ALU.add).then_inc(
                    var_done, 1)

            def normalise(dst, tiles, at):
                dve.wait_ge(rstd_done, at + 1)
                for t in range(SUB):
                    last = nc.vector.tensor_scalar(dst(t), tiles(t), mean[:, t:t + 1], rstd[:, t:t + 1],
                                                   ALU.subtract, ALU.mult)
                last.then_inc(ln_done, 1)

            def x_tile(s):
                return lambda t: X[:, ds(SUB * s + t, 1), :].rearrange("p o d -> p (o d)")

            def mixed_tile(t):
                return mixed[:, t, :]

            def iteration(s, c, finish):
                for k in range(UNITS):
                    if finish and k == 0:
                        dve.wait_ge(words_stored, 2 * s + 1)
                    elif finish and k == 1:
                        dve.wait_ge(words_stored, 2 * s + 2)
                    unpack(s, c, k)
                    unit_low(s, c, k)
                    unit_mask(s, c, k)
                    if finish and s > 0 and k == 0:
                        read_attention(s - 1)
                    if s + 1 < NS:
                        pack(SUB * (s + 1) + c, k)
                        add_pair(s + 1, c, k)
                    if finish and s > 0 and k == 1:
                        dve.wait_ge(attn_read, s)
                        moments_of(mixed_tile, s - 1)
                    if finish and s > 0 and k == 3:
                        normalise(x_tile(s - 1), mixed_tile, s - 1)
                    if finish and s == 0 and k + 1 < UNITS:
                        low_values(k + 1)

            for s in range(NS):
                iteration(s, 0, True)
                with dve.Fori(1, NC) as c:
                    iteration(s, c, False)

            def unpack_late(s, c, begin):
                w = words[:, ds(s, 1), ds(c, 1), :].rearrange("p o a w -> p (o a w)")
                for b in range(BITS):
                    if not begin:
                        dve.wait_ge(mask_used, BITS * (NC * s + c - 1) + b + 1)
                    nc.vector.tensor_scalar(mask[:, b, :], w, 14 - b, 0x4000,
                                            ALU.logical_shift_left, ALU.bitwise_and).then_inc(mask_ready, 1)

            dve.wait_ge(deg_done, 4 * NT)
            nc.vector.tensor_reduce(out=rdeg[:], in_=degree[:], op=ALU.add, axis=AX.X).then_inc(deg_sum, 1)
            dve.wait_ge(deg_sum, 1)
            nc.vector.tensor_scalar(rdeg[:], rdeg[:], 1.0, None, ALU.max).then_inc(deg_max, 1)
            dve.wait_ge(deg_max, 1)
            nc.vector.reciprocal(rdeg[:], rdeg[:]).then_inc(rdeg_done, 1)
            dve.wait_ge(masked, UPS * NS)
            unpack_late(0, 0, True)

            def low_x1(c, b0, b1, at):
                dve.wait_ge(x1_hi, at)
                nc.vector.scalar_tensor_tensor(x1c[:, c, b0:b1, LOW:LOW + D], Xc[:, c, b0:b1, :], X1_SCALE,
                                               x1c[:, c, b0:b1, 0:D], ALU.mult, ALU.subtract).then_inc(x1_split, 1)

            read_attention(NS - 1)
            low_x1(0, 0, BITS - 1, 1)
            dve.wait_ge(attn_read, NS)
            moments_of(mixed_tile, NS - 1)
            normalise(x_tile(NS - 1), mixed_tile, NS - 1)
            dve.wait_ge(ln_done, NS)
            low_x1(0, BITS - 1, BITS, 2)
            for c in range(1, NC):
                low_x1(c, 0, BITS, 2 + c)

            def keep_aggregate(s):
                dve.wait_ge(mask_used, BITS * NC * (s + 1))
                since(dve, feat_done, s)
                nc.vector.tensor_scalar(aggT[:, 1, :], ps[:, 1, :], 1.0 / (MASK_ONE * X1_SCALE), None,
                                        ALU.mult).then_inc(agg_copied, 1)

            def sum_features(s):
                dve.wait_ge(feat_done, s + 1)
                since(dve, ln_done, NS + s)
                nc.vector.tensor_tensor(out=feat, in0=ps[:, 4:8, 0:D],
                                        in1=bias[:].rearrange("p (o d) -> p o d", o=1).broadcast_to([P, SUB, D]),
                                        op=ALU.add).then_inc(feat_b, 1)
                dve.wait_ge(feat_b, s + 1)
                for t in range(SUB):
                    last = nc.vector.scalar_tensor_tensor(feat[:, t, :], ps[:, 4 + t, D:2 * D],
                                                          rdeg[:, ds(SUB * s + t, 1)], feat[:, t, :],
                                                          ALU.mult, ALU.add)
                last.then_inc(feat_sum, 1)
                dve.wait_ge(feat_sum, s + 1)
                nc.vector.scalar_tensor_tensor(feat, feat, 0.0, X[:, ds(SUB * s, SUB), :],
                                               ALU.max, ALU.add).then_inc(feat_res, 1)

            def finish_features(s):
                dve.wait_ge(feat_res, s + 1)
                moments_of(lambda t: feat[:, t, :], NS + s)
                since(dve, stored, 16 * s)
                normalise(lambda t: result[:, t, :], lambda t: feat[:, t, :], NS + s)

            def layer_tile(s, begin):
                if not begin:
                    unpack_late(s, 0, False)
                unpack_late(s, 1, False)
                if not begin:
                    sum_features(s - 1)
                unpack_late(s, 2, False)
                if not begin:
                    finish_features(s - 1)
                unpack_late(s, 3, False)
                keep_aggregate(s)

            layer_tile(0, True)
            with dve.Fori(1, NS) as s:
                layer_tile(s, False)
            sum_features(NS - 1)
            finish_features(NS - 1)


_INS = ['x', 'adj', 'L0_gnn_W', 'L1_gnn_W_self', 'L1_gnn_b_self', 'L1_gnn_W_nb', 'L1_gnn_b_nb',
        'L1_gnn_W_comb', 'L1_gnn_b_comb']


def kernel(**inputs):
    import numpy as _np
    import concourse.bacc as _bacc
    from concourse import mybir as _mybir
    from concourse.bass_utils import run_bass_kernel_spmd as _run

    nc = _bacc.Bacc("TRN2", target_bir_lowering=False, num_devices=1)
    arrays, args = {}, []
    for name in _INS:
        a = _np.ascontiguousarray(inputs[name])
        arrays[f"in_{name}_dram"] = a
        args.append(nc.dram_tensor(f"in_{name}_dram", a.shape, _mybir.dt.from_np(a.dtype), kind="ExternalInput").ap())
    args.append(nc.dram_tensor("out_0_dram", (N, D), _mybir.dt.float32, kind="ExternalOutput").ap())
    gnn_kernel(nc, *args)
    r = _run(nc, [arrays], core_ids=[0])
    return r.results[0]["out_0_dram"]
```

```python
import concourse.bass as bass
from concourse import mybir
from contextlib import ExitStack
import math

N, D, P = 4096, 256, 128
KD = D // P
NT = N // P
SUB = 4
SW = SUB * P
NS = N // SW
BITS = 8
NC = NT // BITS
UNITS = BITS // 2
UPS = NC * UNITS
QUARTER = N // 4
VW = 2 * D + 2
LOW = D + 2
LEAD = 3
RING = 2 * SUB
PACKED = ((1, 2, 2, 2), (1, 1, 1, 2), (1, 1, 1, 1), (1, 1, 1, 1), (0, 1, 1, 1), (0, 1, 1, 1), (0, 1, 1, 0), (0, 0, 0, 0))
EPS_SIM = 1e-8
EPS_M = 1e-30
EPS_LN = 1e-5
SIM_SCALE = 1024.0
VAL_TOP = 8192.0
X1_SCALE = 2048.0
WORD_BIAS = (2 ** BITS - 1) / 2.0
MASK_ONE = 2.0
EXP_BIAS = -1.0 + 13.0 * math.log(2.0)


def gnn_kernel(nc, x, adj, w0, w_self, b_self, w_nb, b_nb, w_comb, b_comb, out):
    f32, f16, bf16 = mybir.dt.float32, mybir.dt.float16, mybir.dt.bfloat16
    u16, u8, i32 = mybir.dt.uint16, mybir.dt.uint8, mybir.dt.int32
    ALU, ACT, AX = mybir.AluOpType, mybir.ActivationFunctionType, mybir.AxisListType
    ds = bass.ds

    ctx = ExitStack()
    with ctx:
        def sb(name, shape, dt):
            return ctx.enter_context(nc.sbuf_tensor(name, shape, dt))

        def sem(name):
            return ctx.enter_context(nc.semaphore(name))

        X = sb("X", [P, NT, D], f32)
        similar = sb("similar", [P, 2, KD, N], f16)
        values = sb("values", [P, NT, VW], f16)
        words = sb("words", [P, NS, NC, SW], u16)
        mask = sb("mask", [P, BITS, SW], u16)
        adj_in = sb("adj_in", [P, 2, QUARTER], i32)
        signs = sb("signs", [P, 2, QUARTER], bf16)
        weighed = sb("weighed", [P, 2, SW], bf16)
        exps_split = sb("exps_split", [P, 2, 2, SUB, 2, P], f16)
        mirror_in = sb("mirror_in", [P, 2, 2, 2, SW], f16)
        row_words = sb("row_words", [P, RING, SW], bf16)
        Ph = sb("Ph", [P, UNITS, 2, SW], f16)
        Pl = sb("Pl", [P, UNITS, 2, SW], f16)
        M1 = sb("M1", [P, KD, D], f32)
        M2 = sb("M2", [P, KD, D], f32)
        bias = sb("bias", [P, D], f32)
        ident32 = sb("ident32", [P, P], f32)
        ident16 = sb("ident16", [P, P], f16)
        identb = sb("identb", [P, P], bf16)
        diag2 = sb("diag2", [P, P], f16)
        square_junk = sb("square_junk", [P, SUB * D], u8)
        bcol = sb("bcol", [P, 2 * KD], f32)
        norm2 = sb("norm2", [P, NT], f32)
        rnorm = sb("rnorm", [P, SUB], f32)
        mixed = sb("mixed", [P, SUB, D], f32)
        minus_half = sb("minus_half", [P, SUB], f32)
        plus_half = sb("plus_half", [P, 1], f32)
        big = sb("big", [P, 4], f32)
        msum = sb("msum", [P, 2], f32)
        mscale = sb("mscale", [P, 4], f32)
        exp_bias = sb("exp_bias", [P, 1], f32)
        degree = sb("degree", [P, NT, 4], f32)
        rdeg = sb("rdeg", [P, NT], f32)
        rsum = sb("rsum", [P, SUB], f32)
        stats = sb("stats", [P, SUB, 6], f32)
        mean_sum, mean_gap, gap2, squares, mean = (
            sb(n, [P, SUB], f32) for n in ("mean_sum", "mean_gap", "gap2", "squares", "mean"))
        rstd = sb("rstd", [P, SUB], f32)
        stage = row_words[:, SUB:RING, :].rearrange("p t w -> p (t w)").bitcast(f32).rearrange(
            "p (t d) -> p t d", d=D)

        Wh = words[:, :, :, :].rearrange("p s c w -> p (s c w)").bitcast(f32).rearrange(
            "p (t d) -> p t d", d=D)
        wst = Ph[:, :, :, :].rearrange("p q k w -> p (q k w)").bitcast(f32).rearrange(
            "p (a d) -> p a d", d=D)
        w0_in, wself_in, wnb_in, wcomb_in = (
            wst[:, 0:2, :], wst[:, 2:4, :], wst[:, 4:6, :], mixed[:, :, :])
        wstT = Pl[:, :, :, :].rearrange("p q k w -> p (q k w)").bitcast(f32).rearrange(
            "p (a d) -> p a d", d=D)
        w0T, wselfT, wnbT = wstT[:, 0:2, :], wstT[:, 2:4, :], wstT[:, 4:6, :]
        bcomb_in = wst[:, 6, :]
        bcast = wstT[:, 6:8, :].rearrange("p a (b n) -> p (a b) n", n=P)
        mask_flat = mask[:, :, :].rearrange("p b w -> p (b w)")
        mirror_flat = mirror_in[:, :, :, :, :].rearrange("p b k h n -> p (b k h n)")
        xT = [m.bitcast(f32).rearrange("p (t k n) -> p t k n", t=SUB, k=KD)
              for m in (mask_flat[:, 0:4 * SW], mirror_flat[:, 0:4 * SW])]
        unit = mask_flat[:, 4 * SW:8 * SW].bitcast(f16).rearrange("p (h t d) -> p h t d", h=2, t=SUB)
        x_stage = [stage[:, :, :], mirror_flat[:, 4 * SW:8 * SW].bitcast(f32).rearrange("p (t d) -> p t d", d=D)]
        mask16 = mask_flat.bitcast(f16).rearrange("p (b w) -> p b w", w=SW)
        x1s = values
        Xc = X[:, :, :].rearrange("p (b c) d -> p c b d", c=NC)
        x1c = x1s[:, :, :].rearrange("p (b c) d -> p c b d", c=NC)
        late = similar[:, :, :, :].rearrange("p h k n -> p (h k n)").bitcast(f32)
        aggT = late[:, 0:1024].bitcast(f16).rearrange("p (h k n) -> p h k n", h=2, k=KD)
        x1T = late[:, 1024:2048].bitcast(f16).rearrange("p (h k n) -> p h k n", h=2, k=KD)
        Ms = adj_in[:, 0, :].bitcast(f16).rearrange("p (m h k d) -> p m h k d", m=2, h=2, k=KD)
        feat = late[:, 2048:3072].rearrange("p (t d) -> p t d", d=D)
        result = late[:, 3072:4096].rearrange("p (t d) -> p t d", d=D)

        ps = ctx.enter_context(nc.psum_tensor("ps", [P, 8, 512], f32))
        ps_flat = ps[:, :, :].rearrange("p b w -> p (b w)")
        sim_ps = [ps_flat[:, 0:1024], ps_flat[:, 1024:2048]]
        word_ps = sim_ps[1].bitcast(bf16)
        wh_ps = [ps_flat[:, 1024:2048], ps_flat[:, 2048:3072]]
        out_ps = ps[:, 4:8, :]

        kept = nc.dram_tensor("kept_exps", (NS, NC, NS, NC, P, 2, P), f16, kind="Internal").ap()

        x_in, w_in, wc_in = sem("x_in"), sem("w_in"), sem("wc_in")
        w0_ready = sem("w0_ready")
        consts, ln_done = sem("consts"), sem("layernorm_done")
        staged = [sem("staged0"), sem("staged1")]
        pool_step = sem("pool_step")
        w_t, w_tc = sem("w_transposed"), sem("w_copied")
        bc_done, fused, fused_copied = sem("bias_columns"), sem("weights_fused"), sem("fused_copied")
        xt_done, xt_copied = sem("x_transposed"), sem("x_copied")
        wh_done, wh_copied, sq_done = sem("wh_done"), sem("wh_copied"), sem("squares_done")
        n2_done, rn_done = sem("norm2_done"), sem("rnorm_done")
        unit_hi, unit_done = sem("unit_high"), sem("unit_done")
        ut_done, ut_copied = sem("unit_transposed"), sem("unit_copied")
        top_done, max_done, all_max, scale_done, vscale_done = (
            sem("row_max_done"), sem("max_done"), sem("all_max"), sem("scale_done"), sem("vscale_done"))
        msq_done, m_steps, msum_done, msum_all, mpow_done, mscale_done, m_hi, m_split = (
            sem("m_squares_done"), sem("m_steps"), sem("m_sums_done"), sem("m_sums_all"), sem("m_powers_done"), sem("mscale_done"),
            sem("m_high"), sem("m_split"))
        agg_hi, agg_hi1 = sem("agg_high"), sem("agg_high1")
        vh_done, vl_done = sem("values_high"), sem("values_low")
        adj_ready = [sem("adj_ready0"), sem("adj_ready1")]
        signed, scaled, summed, packed = sem("signed"), sem("scaled"), sem("quarters_summed"), sem("rows_packed")
        kept_done = {b: sem(f"kept_done{b}") for b in range(1, NS)}
        mirror_ready = {b: sem(f"mirror_ready{b}") for b in range(NS - 1)}
        words_t, words_first, words_rest = sem("words_transposed"), sem("words_first"), sem("words_rest")
        unpacked, diag_done = sem("unpacked"), sem("diag_done")
        sims, exps, highs, lows, masked, attended = (
            sem("sims"), sem("exps"), sem("highs"), sem("lows"), sem("masked"), sem("attended"))
        rs_done, rs_scaled, attn_read = sem("rsum_done"), sem("rsum_scaled"), sem("attn_read")
        st_done, parts_done, var_done, rstd_done = (
            sem("stats_done"), sem("moment_parts"), sem("variance_done"), sem("rstd_done"))
        deg_sum, deg_max, rdeg_done = sem("deg_sum"), sem("deg_max"), sem("rdeg_done")
        x1_hi, x1_split = sem("x1_high"), sem("x1_split")
        mask_ready, mask_used = sem("mask_ready"), sem("mask_used")
        agg_copied = sem("agg_copied")
        x1t_done, x1t_copied, own_done = sem("x1_transposed"), sem("x1t_copied"), sem("own_features_done")
        feat_done, feat_b, feat_sum, feat_res = (
            sem("features_done"), sem("features_biased"), sem("features_summed"), sem("features_residual"))
        stored = sem("stored")

        block = ctx.enter_context(nc.Block())

        def since(eng, s, v):
            if not (isinstance(v, int) and v <= 0):
                eng.wait_ge(s, v)

        def pair_of(k):
            return UNITS - 1 - k % UNITS

        def computed(s, k):
            return [kk for kk in range(2) if 2 * pair_of(k) + kk >= s]

        def mirrored(s, k):
            return [kk for kk in range(2) if 2 * pair_of(k) + kk < s]

        def kept_blocks(s, k):
            return [2 * pair_of(k) + kk for kk in computed(s, k) if 2 * pair_of(k) + kk > s]

        def last_in_buffer(s, c, k):
            if k >= 2:
                return s, c, k - 2
            if isinstance(c, int) and c == 0:
                s, c = s - 1, NC
            if s < 0:
                return None
            users = [i for i in (k, k + 2) if computed(s, i)]
            return (s, c - 1, max(users)) if users else None

        def last_mirror(s, c, k):
            if k >= 2 and mirrored(s, k - 2):
                return s, c, k - 2
            if isinstance(c, int) and c == 0:
                s, c = s - 1, NC
            users = [i for i in range(UNITS) if s >= 0 and i % 2 == k % 2 and mirrored(s, i)]
            return (s, c - 1, max(users)) if users else None

        def units_computed(s):
            return sum(1 for k in range(UNITS) if computed(s, k))

        def computed_before(s, c, k):
            return NC * sum(units_computed(i) for i in range(s)) + units_computed(s) * c + k

        def tiles_packed(s, c, c0):
            n = PACKED[s][c0]
            first = SUB + sum(sum(PACKED[i]) for i in range(s)) + sum(PACKED[s][:c0])
            return [first + n * (c - c0) + i for i in range(n)]

        def quarters_packed(s, c, c0, k):
            tiles = tiles_packed(s, c, c0)
            return [(tiles[j // 4], j % 4) for j in range(len(tiles) * k, len(tiles) * (k + 1))]

        def spans(s):
            def alike(c):
                last, now = tiles_packed(s, c - 1, c - 1), tiles_packed(s, c, c)
                return len(last) == len(now) and (not now or last[0] // RING == now[-1] // RING)
            ends = [c for c in range(2, NC) if not alike(c)] + [NC]
            return list(zip([1] + ends[:-1], ends))

        def over_c(eng, s, body):
            for c0, c1 in spans(s):
                if c1 - c0 == 1:
                    body(c0, c0)
                else:
                    with eng.Fori(c0, c1) as c:
                        body(c, c0)

        VALUE_ORDER = [0] + list(range(NS - 1, 0, -1))

        def value_groups(k):
            return [(at, g) for at, g in enumerate(VALUE_ORDER)
                    if (g // 2 == pair_of(k) if g else k == 0)]

        def values_split(k):
            return sum(len(value_groups(i)) for i in range(k + 1))

        def computed_until(s, c, k):
            before = last_in_buffer(s, c, k)
            return computed_before(*before) + 1 if before else 0

        def unit_at(s, c, k):
            return UPS * s + UNITS * c + k

        def quarter(tile, r):
            return 4 * tile + r + 1

        @block.sync
        def _(sp):
            xv = x.rearrange("(t p) d -> p t d", p=P)

            def load_adj(tile, r):
                sp.dma_start(adj_in[:, r % 2, :],
                             adj[ds(tile * P, P), r * QUARTER:(r + 1) * QUARTER]).then_inc(adj_ready[r % 2], 16)

            def next_adj(tile, r):
                sp.wait_ge(signed, quarter(tile, r))
                load_adj(tile if r < 2 else tile + 1, (r + 2) % 4)

            def stage_x(g, odd):
                since(sp, xt_done, g - 1)
                sp.dma_start(x_stage[odd], xv[:, ds(g * SUB, SUB), :]).then_inc(staged[odd], 16)

            stage_x(0, 0)
            stage_x(1, 1)
            load_adj(0, 0)
            load_adj(0, 1)
            with sp.Fori(0, NS // 2 - 1) as i:
                for odd in range(2):
                    stage_x(2 * i + 2 + odd, odd)
                    next_adj(i, 2 * odd)
                    next_adj(i, 2 * odd + 1)
            for r in range(4):
                next_adj(NS // 2 - 1, r)

            def load_mirror(s, c, k):
                for kk in mirrored(s, k):
                    b = 2 * pair_of(k) + kk
                    user = last_mirror(s, c, k)
                    if user:
                        sp.wait_ge(masked, unit_at(*user) + 1)
                    sp.wait_ge(kept_done[s], 16 * NC * s)
                    sp.dma_start_transpose(
                        mirror_in[:, k % 2, kk, :, :],
                        kept[b, ds(c, 1), s, :, :, :, :].rearrange("o r p h n -> (o r p) (h n)")).then_inc(
                            mirror_ready[b], 16)

            def keep_exps(s, c, k):
                for kk in computed(s, k):
                    b = 2 * pair_of(k) + kk
                    if b > s:
                        sp.wait_ge(lows, computed_before(s, c, k) + 1)
                        sp.dma_start(kept[s, :, b, ds(c, 1), :, :, :].rearrange("t o p h n -> p t (o h n)"),
                                     exps_split[:, k % 2, kk, :, :, :].rearrange("p t h n -> p t (h n)")).then_inc(
                                         kept_done[b], 16)

            def traffic(s, c, c0):
                end = isinstance(c, int) and c == NC - 1
                if s == 0:
                    some = NT // NC
                    sp.dma_start(X[:, ds(c * some, some), :], xv[:, ds(c * some, some), :]).then_inc(x_in, 16)
                for k in range(UNITS):
                    for tile, q in quarters_packed(s, c, c0, k):
                        if not (isinstance(tile, int) and tile == NT - 1 and q >= 2):
                            next_adj(tile, q)
                    if k + 2 < UNITS and not mirrored(s, k):
                        load_mirror(s, c, k + 2)
                    keep_exps(s, c, k)
                    if k + 2 < UNITS and mirrored(s, k):
                        load_mirror(s, c, k + 2)
                    if k + 2 >= UNITS and not end:
                        load_mirror(s, c + 1, k - 2)
                    elif k + 2 >= UNITS and s + 1 < NS:
                        load_mirror(s + 1, 0, k - 2)

            for s in range(NS):
                traffic(s, 0, 0)
                for c0, c1 in spans(s):
                    apart = c1 == NC or s == NS - 2
                    if c1 - apart - c0 == 1:
                        traffic(s, c0, c0)
                    elif c1 - apart > c0:
                        with sp.Fori(c0, c1 - apart) as c:
                            traffic(s, c, c0)
                    if apart:
                        traffic(s, c1 - 1, c0)

            def store(s):
                sp.wait_ge(ln_done, NS + s + 1)
                sp.dma_start(out[ds(s * SW, SW), :].rearrange("(t p) d -> p t d", p=P),
                             result).then_inc(stored, 16)

            with sp.Fori(0, NS) as s:
                store(s)
            sp.wait_ge(stored, 16 * NS)

        @block.gpsimd
        def _(pool):
            for t in (ident32, ident16, identb, diag2):
                nc.gpsimd.memset(t[:], 0.0)
            nc.gpsimd.memset(minus_half[:], -0.5)
            nc.gpsimd.memset(plus_half[:], 0.5)
            nc.gpsimd.memset(exp_bias[:], EXP_BIAS).then_inc(pool_step, 1)
            pool.wait_ge(pool_step, 1)
            for t, one in ((ident32, 1.0), (ident16, 1.0), (identb, 1.0), (diag2, MASK_ONE)):
                last = nc.gpsimd.affine_select(out=t[:], in_=t[:], compare_op=ALU.not_equal, fill=one, base=0,
                                               pattern=[[-1, P]], channel_multiplier=1)
            last.then_inc(consts, 1)

            with pool.Fori(0, NS) as g:
                pool.wait_ge(n2_done, g + 1)
                nc.gpsimd.tensor_tensor(out=rnorm[:], in0=rnorm[:], in1=minus_half[:], op=ALU.pow).then_inc(rn_done, 1)
            pool.wait_ge(max_done, 1)
            nc.gpsimd.partition_all_reduce(big[:, 1:2], big[:, 0:1], P, bass.bass_isa.ReduceOp.max).then_inc(all_max, 1)
            pool.wait_ge(all_max, 1)
            nc.gpsimd.tensor_tensor(out=big[:, 2:3], in0=big[:, 1:2], in1=minus_half[:, 0:1], op=ALU.pow)
            nc.gpsimd.tensor_tensor(out=big[:, 3:4], in0=big[:, 1:2], in1=plus_half[:], op=ALU.pow).then_inc(
                scale_done, 1)
            pool.wait_ge(msum_done, 1)
            nc.gpsimd.partition_all_reduce(mscale[:, 1:2], mscale[:, 0:1], P, bass.bass_isa.ReduceOp.max).then_inc(
                msum_all, 1)
            pool.wait_ge(msum_all, 1)
            nc.gpsimd.tensor_tensor(out=mscale[:, 2:3], in0=mscale[:, 1:2], in1=plus_half[:], op=ALU.pow)
            nc.gpsimd.tensor_tensor(out=mscale[:, 1:2], in0=mscale[:, 1:2], in1=minus_half[:, 0:1],
                                    op=ALU.pow).then_inc(mpow_done, 1)
            with pool.Fori(0, 2 * NS) as at:
                pool.wait_ge(var_done, at + 1)
                nc.gpsimd.tensor_tensor(out=rstd[:], in0=rstd[:], in1=minus_half[:], op=ALU.pow).then_inc(
                    rstd_done, 1)

        @block.tensor
        def _(pe):
            def transpose_weights(bank, w):
                for ko in range(KD):
                    for ki in range(KD):
                        last = nc.tensor.transpose(ps[:, bank, ki * D + ko * P:ki * D + (ko + 1) * P],
                                                   w[:, ko, ki * P:(ki + 1) * P], ident32[:])
                last.then_inc(w_t, 1)

            pe.wait_ge(consts, 1)
            pe.wait_ge(w0_ready, 16)
            transpose_weights(4, w0_in)

            def transpose_x(g, odd):
                since(pe, xt_copied, g)
                pe.wait_ge(staged[odd], 8 * (g - odd) + 16)
                for t in range(SUB):
                    for k in range(KD):
                        at = (t * KD + k) * P
                        last = nc.tensor.transpose(ps_flat[:, at:at + P],
                                                   x_stage[odd][:, t, k * P:(k + 1) * P], ident32[:])
                last.then_inc(xt_done, 1)

            def project(g, odd):
                pe.wait_ge(xt_copied, g + 1)
                pe.wait_ge(w_tc, 1)
                since(pe, wh_copied, g - 1)
                for t in range(SUB):
                    for k in range(KD):
                        last = nc.tensor.matmul(wh_ps[odd][:, t * D:(t + 1) * D], xT[odd][:, t, k, :],
                                                w0T[:, k, :], start=(k == 0), stop=(k == KD - 1))
                last.then_inc(wh_done, 1)

            def transpose_unit(g):
                pe.wait_ge(unit_done, g + 1)
                since(pe, ut_copied, g)
                dst = ps_flat[:, 3072:4096].bitcast(f16)
                for h in range(2):
                    for k in range(KD):
                        for t in range(SUB):
                            at = (h * KD + k) * SW + t * P
                            last = nc.tensor.transpose(dst[:, at:at + P], unit[:, h, t, k * P:(k + 1) * P],
                                                       ident16[:])
                last.then_inc(ut_done, 1)

            transpose_x(0, 0)
            project(0, 0)
            pe.wait_ge(w_in, 16 * 2)
            transpose_weights(6, wself_in)
            transpose_weights(7, wnb_in)
            transpose_x(1, 1)
            pe.wait_ge(w_tc, 3)

            def two_groups(i):
                for odd in range(2):
                    g = 2 * i + 1 + odd
                    transpose_x(g + 1, odd)
                    project(g, 1 - odd)
                    transpose_unit(g - 1)

            two_groups(0)
            with pe.Fori(1, NS // 2 - 1) as i:
                two_groups(i)
            project(NS - 1, 1)
            transpose_unit(NS - 2)
            pe.wait_ge(wc_in, 16 * 6)
            pe.wait_ge(bc_done, 1)
            pe.wait_ge(wh_copied, NS - 1)
            for i, wT in enumerate((wselfT, wnbT)):
                for kd in range(KD):
                    for km in range(KD):
                        nc.tensor.matmul(ps[:, 2 + i, kd * D:(kd + 1) * D], wT[:, km, kd * P:(kd + 1) * P],
                                         wcomb_in[:, KD * i + km, :], start=(km == 0), stop=(km == KD - 1))
            pe.wait_ge(wh_copied, NS)
            for k in range(2 * KD):
                last = nc.tensor.matmul(ps[:, 4, 0:D], bcast[:, k, :], wcomb_in[:, k, :],
                                        start=(k == 0), stop=(k == 2 * KD - 1))
            last.then_inc(fused, 1)

            transpose_unit(NS - 1)

            def similarities(s, c, k):
                if not computed(s, k):
                    return
                since(pe, lows, computed_until(s, c, k))
                for kk in computed(s, k):
                    jb = NC * (2 * pair_of(k) + kk) + c
                    terms = [(hj, hi, d) for hj, hi in ((0, 0), (0, 1), (1, 0)) for d in range(KD)]
                    for i, (hj, hi, d) in enumerate(terms):
                        last = nc.tensor.matmul(sim_ps[k % 2][:, kk * SW:(kk + 1) * SW],
                                                similar[:, hj, d, ds(jb * P, P)],
                                                similar[:, hi, d, s * SW:(s + 1) * SW],
                                                start=(i == 0), stop=(i == len(terms) - 1))
                last.then_inc(sims, 1)

            def attend(s, c, k):
                n = unit_at(s, c, k)
                first = isinstance(c, int) and c == 0 and k == 0
                end = isinstance(c, int) and c == NC - 1 and k == UNITS - 1
                pe.wait_ge(masked, n + 1)
                if s == 0 and isinstance(c, int) and c == 0:
                    pe.wait_ge(vl_done, values_split(k))
                for kk in range(2):
                    jb = NC * (2 * pair_of(k) + kk) + c
                    row = values[:, ds(jb, 1), :].rearrange("p o w -> p (o w)")
                    for t in range(SUB):
                        if first and kk == 0 and s > 0:
                            pe.wait_ge(attn_read, SUB * (s - 1) + t + 1)
                        hi = Ph[:, k, kk, t * P:(t + 1) * P]
                        lo = Pl[:, k, kk, t * P:(t + 1) * P]
                        nc.tensor.matmul(out_ps[:, t, 0:D + 1], hi, row[:, 0:D + 1],
                                         start=first and kk == 0, stop=False, skip_group_check=True)
                        nc.tensor.matmul(out_ps[:, t, 0:D], hi, row[:, LOW:LOW + D],
                                         start=False, stop=False, skip_group_check=True)
                        last = nc.tensor.matmul(out_ps[:, t, 0:D + 1], lo, row[:, 0:D + 1],
                                                start=False, stop=end and kk == 1, skip_group_check=True)
                last.then_inc(attended, 1)

            def transpose_words(s):
                pe.wait_ge(packed, SUB * (s + 1))
                since(pe, lows, computed_until(s, 0, 1))
                since(pe, words_rest, s)
                for t in range(SUB):
                    for c in range(NC):
                        last = nc.tensor.transpose(word_ps[:, c * SW + t * P:c * SW + (t + 1) * P],
                                                   row_words[:, SUB * (s % 2) + t, c * P:(c + 1) * P], identb[:])
                last.then_inc(words_t, 1)

            def attend_behind(s, c, q):
                if q >= LEAD:
                    attend(s, c, q - LEAD)
                elif isinstance(c, int) and c == 0:
                    if s > 0:
                        attend(s - 1, NC - 1, q - LEAD + UNITS)
                else:
                    attend(s, c - 1, q - LEAD + UNITS)

            def attention_tile(s):
                early = s > 0 and not computed(s - 1, UNITS - 1)
                if early:
                    transpose_words(s)
                if s == 0:
                    pe.wait_ge(ut_copied, NS)
                similarities(s, 0, 0)
                attend_behind(s, 0, 0)
                if s == 0:
                    pe.wait_ge(fused_copied, 2)
                if not early:
                    transpose_words(s)
                    attend_behind(s, 0, 1)
                if computed(s, 1):
                    pe.wait_ge(words_first, s + 1)
                    pe.wait_ge(words_rest, s + 1)
                similarities(s, 0, 1)
                if early:
                    attend_behind(s, 0, 1)
                for q in range(2, UNITS):
                    similarities(s, 0, q)
                    attend_behind(s, 0, q)
                with pe.Fori(1, NC) as c:
                    for q in range(UNITS):
                        similarities(s, c, q)
                        attend_behind(s, c, q)

            for s in range(NS):
                attention_tile(s)
            for k in range(UNITS - LEAD, UNITS):
                attend(NS - 1, NC - 1, k)

            def aggregate(s, c, bs=range(BITS), ready=None, start=None):
                first = isinstance(c, int) and c == 0 if start is None else start
                end = isinstance(c, int) and c == NC - 1
                for b in bs:
                    pe.wait_ge(mask_ready, BITS * (NC * s + c) + b + 1 if ready is None else ready)
                    for k in range(KD):
                        for h in range(2):
                            jb = NC * b + c
                            at = (LOW if h else 0) + k * P
                            last = nc.tensor.matmul(ps[:, k, :],
                                                    x1s[:, ds(jb, 1), at:at + P].rearrange("p o n -> p (o n)"),
                                                    mask16[:, b, :],
                                                    start=first and b == 0 and h == 0,
                                                    stop=end and b == BITS - 1 and h == 1, skip_group_check=True)
                    last.then_inc(mask_used, 1)

            def aggregate_first():
                most = range(BITS - 1)
                pe.wait_ge(x1_split, 1)
                aggregate(0, 0, most)
                pe.wait_ge(x1_split, 2)
                aggregate(0, 1, most)
                pe.wait_ge(x1_split, 4)
                aggregate(0, 0, [BITS - 1])
                aggregate(0, 1, [BITS - 1])
                aggregate(0, 2)
                pe.wait_ge(x1_split, 5)

            def transpose_x1(s):
                since(pe, x1t_copied, s)
                dst = ps_flat[:, 1024:2048].bitcast(f16)
                for h in range(2):
                    for k in range(KD):
                        for t in range(SUB):
                            at = (h * KD + k) * SW + t * P
                            col = (LOW if h else 0) + k * P
                            last = nc.tensor.transpose(
                                dst[:, at:at + P],
                                x1s[:, ds(SUB * s + t, 1), col:col + P].rearrange("p o n -> p (o n)"), ident16[:])
                last.then_inc(x1t_done, 1)

            def times_m(out, operand, t, m):
                terms = [(ho, hm, k) for ho, hm in ((0, 0), (0, 1), (1, 0)) for k in range(KD)]
                for i, (ho, hm, k) in enumerate(terms):
                    last = nc.tensor.matmul(out, operand[:, ho, k, t * P:(t + 1) * P], Ms[:, m, hm, k, :],
                                            start=(i == 0), stop=(i == len(terms) - 1))
                return last

            def own_features(s):
                pe.wait_ge(x1t_copied, s + 1)
                pe.wait_ge(m_split, 1)
                since(pe, feat_sum, SUB * s)
                for t in range(SUB):
                    last = times_m(ps[:, 4 + t, 0:D], x1T, t, 0)
                last.then_inc(own_done, 1)

            def neighbour_features(s):
                pe.wait_ge(agg_copied, s + 1)
                pe.wait_ge(feat_b, s + 1)
                for t in range(SUB):
                    times_m(ps[:, 4 + t, D:2 * D], aggT, t, 1).then_inc(feat_done, 1)

            def finish_tile(s):
                transpose_x1(s)
                aggregate(s, NC - 1)
                own_features(s)

            aggregate_first()
            finish_tile(0)
            with pe.Fori(1, NS) as s:
                pe.wait_ge(agg_copied, s)
                aggregate(s, 0)
                neighbour_features(s - 1)
                with pe.Fori(1, NC - 1) as c:
                    aggregate(s, c)
                finish_tile(s)
            neighbour_features(NS - 1)

        @block.scalar
        def _(act):
            def rows(w):
                return w.rearrange("(k p) d -> p k d", p=P)
            act.dma_start(w0_in, rows(w0)).then_inc(w0_ready, 16)
            for dst, w in ((wself_in, w_self), (wnb_in, w_nb)):
                act.dma_start(dst, rows(w)).then_inc(w_in, 16)
            act.dma_start(wcomb_in, rows(w_comb)).then_inc(wc_in, 16)
            for i, b in enumerate((b_self, b_nb)):
                for k in range(KD):
                    act.dma_start(bcol[:, KD * i + k:KD * i + k + 1],
                                  b[k * P:(k + 1) * P].rearrange("(p o) -> p o", o=1)).then_inc(wc_in, 16)
            act.dma_start(bcomb_in, b_comb.rearrange("(o d) -> o d", o=1).broadcast_to([P, D])).then_inc(wc_in, 16)


            for i, wT in enumerate((wselfT, wnbT)):
                act.wait_ge(w_t, 2 + i)
                nc.scalar.copy(wT, ps[:, 6 + i, :].rearrange("p (k d) -> p k d", k=KD)).then_inc(w_tc, 1)

            def keep_wh(g, odd):
                act.wait_ge(wh_done, g + 1)
                since(act, sq_done, g)
                for t in range(SUB):
                    last = nc.scalar.activation(square_junk[:, t * D:(t + 1) * D], wh_ps[odd][:, t * D:(t + 1) * D],
                                                ACT.Square, accum_out=norm2[:, ds(g * SUB + t, 1)])
                last.then_inc(sq_done, 1)
                nc.scalar.copy(Wh[:, ds(g * SUB, SUB), :],
                               wh_ps[odd].rearrange("p (t d) -> p t d", d=D)).then_inc(wh_copied, 1)

            def keep_unit(g):
                act.wait_ge(ut_done, g + 1)
                nc.scalar.copy(similar[:, :, :, ds(g * SW, SW)].rearrange("p h k n -> p (h k) n"),
                               ps_flat[:, 3072:4096].bitcast(f16).rearrange("p (a n) -> p a n", a=2 * KD)).then_inc(
                                   ut_copied, 1)

            def take_signs(tile, r):
                act.wait_ge(adj_ready[r % 2], 16 * (2 * tile + r // 2) + 16)
                since(act, summed, 3 * tile + (-1, 0, 1, 1)[r])
                nc.scalar.activation(signs[:, r % 2, :], adj_in[:, r % 2, :], ACT.Sign, bias=minus_half[:, 0:1],
                                     accum_out=degree[:, ds(tile, 1), r:r + 1].rearrange("p o h -> p (o h)")
                                     ).then_inc(signed, 1)

            act.wait_ge(consts, 1)
            for r in range(2):
                take_signs(0, r)
            keep_wh(0, 0)
            with act.Fori(0, NS // 2 - 1) as i:
                for odd in range(2):
                    g = 2 * i + 1 + odd
                    take_signs(i + odd, 2 - 2 * odd)
                    take_signs(i + odd, 3 - 2 * odd)
                    keep_wh(g, 1 - odd)
                    keep_unit(g - 1)
            take_signs(SUB - 1, 2)
            take_signs(SUB - 1, 3)
            keep_wh(NS - 1, 1)
            keep_unit(NS - 2)
            act.wait_ge(fused, 1)
            nc.scalar.copy(M1[:, :, :], ps[:, 2, :].rearrange("p (k d) -> p k d", k=KD))
            nc.scalar.copy(M2[:, :, :], ps[:, 3, :].rearrange("p (k d) -> p k d", k=KD)).then_inc(fused_copied, 1)
            keep_unit(NS - 1)
            def high_values(k):
                for _, g in value_groups(k):
                    nc.scalar.activation(values[:, g * SUB:(g + 1) * SUB, 0:D], Wh[:, g * SUB:(g + 1) * SUB, :],
                                         ACT.Copy, scale=big[:, 2:3]).then_inc(vh_done, 1)

            act.wait_ge(vscale_done, 1)
            high_values(0)

            def unit_exps(s, c, k):
                kks = computed(s, k)
                if not kks:
                    return
                f = computed_before(s, c, k)
                z = sim_ps[k % 2][:, kks[0] * SW:2 * SW]
                act.wait_ge(sims, f + 1)
                nc.scalar.activation(z, z, ACT.Exp, bias=exp_bias[:], scale=1.0 / SIM_SCALE ** 2).then_inc(exps, 1)
                act.wait_ge(exps, f + 1)
                since(act, masked, unit_at(s, c, k) - 1)
                before = last_in_buffer(s, c, k)
                if before:
                    s0, c0, k0 = before
                    for b in kept_blocks(s0, k0):
                        act.wait_ge(kept_done[b], 16 * (NC * s0 + c0 + 1))
                nc.scalar.copy(exps_split[:, k % 2, kks[0]:2, :, 0, :].rearrange("p k t n -> p (k t) n"),
                               z.rearrange("p (t n) -> p t n", n=P)).then_inc(highs, 1)

            def iteration(s, c, c0, begin):
                for k in range(UNITS):
                    if begin and k == 0:
                        act.wait_ge(words_t, s + 1)
                        act.wait_ge(vl_done, NS if s else 1)
                        nc.scalar.activation(words[:, s, 0, :], word_ps[:, 0:SW], ACT.Copy, bias=WORD_BIAS,
                                             scale=0.5).then_inc(words_first, 1)
                    unit_exps(s, c, k)
                    if begin and s == 0 and k + 1 < UNITS:
                        high_values(k + 1)
                    for tile, q in quarters_packed(s, c, c0, k):
                        take_signs(tile, q)

            def high_x1(c, b1):
                nc.scalar.mul(x1c[:, ds(c, 1), 0:b1, 0:D].rearrange("p o b d -> p (o b) d"),
                              Xc[:, ds(c, 1), 0:b1, :].rearrange("p o b d -> p (o b) d"), X1_SCALE).then_inc(x1_hi, 1)

            def last_iteration(c, c0):
                iteration(NS - 1, c, c0, False)
                act.wait_ge(attended, unit_at(NS - 1, c, 0))
                act.wait_ge(ln_done, NS - 1)
                high_x1(c - 1, BITS - 1)

            for s in range(NS):
                iteration(s, 0, 0, True)
                if s == 0:
                    act.wait_ge(fused_copied, 2)
                    for i, M in enumerate((M1, M2)):
                        last = nc.scalar.activation(square_junk[:, i * KD * D:(i + 1) * KD * D],
                                                    M[:, :, :].rearrange("p k d -> p (k d)"),
                                                    ACT.Square, accum_out=msum[:, i:i + 1])
                    last.then_inc(msq_done, 1)
                over_c(act, s, last_iteration if s == NS - 1 else lambda c, c0: iteration(s, c, c0, False))

            act.wait_ge(attended, UPS * NS)
            high_x1(NC - 1, BITS - 1)
            act.wait_ge(ln_done, NS)
            nc.scalar.mul(x1s[:, NT - SUB:NT, 0:D], X[:, NT - SUB:NT, :], X1_SCALE).then_inc(x1_hi, 1)

            act.wait_ge(signed, 4 * NT)
            act.wait_ge(mscale_done, 1)
            for i, M in enumerate((M1, M2)):
                last = nc.scalar.activation(Ms[:, i, 0, :, :], M[:, :, :], ACT.Copy, scale=mscale[:, 1:2])
            last.then_inc(m_hi, 1)

            def keep_layer_operands(s):
                act.wait_ge(x1t_done, s + 1)
                since(act, own_done, s)
                nc.scalar.copy(x1T, ps_flat[:, 1024:2048].bitcast(f16).rearrange(
                    "p (h k n) -> p h k n", h=2, k=KD)).then_inc(x1t_copied, 1)
                act.wait_ge(mask_used, BITS * NC * (s + 1))
                since(act, feat_done, SUB * s)
                nc.scalar.mul(aggT[:, 0, 0, :], ps[:, 0, :], 1.0 / (MASK_ONE * X1_SCALE)).then_inc(agg_hi, 1)

            keep_layer_operands(0)
            with act.Fori(1, NS) as s:
                keep_layer_operands(s)

        @block.vector
        def _(dve):
            dve.wait_ge(w_t, 1)
            nc.vector.tensor_copy(w0T, ps[:, 4, :].rearrange("p (k d) -> p k d", k=KD)).then_inc(w_tc, 1)
            nc.vector.memset(values[:, :, D:D + 2], 1.0)

            def copy_xt(g, odd):
                dve.wait_ge(xt_done, g + 1)
                since(dve, wh_done, g - 1)
                nc.vector.tensor_copy(xT[odd], ps_flat[:, 0:1024].rearrange("p (t k n) -> p t k n", t=SUB, k=KD)).then_inc(
                    xt_copied, 1)

            def guard_norms(g):
                dve.wait_ge(sq_done, g + 1)
                since(dve, unit_done, g)
                nc.vector.tensor_scalar(rnorm[:], norm2[:, ds(g * SUB, SUB)], EPS_SIM, 1.0 / SIM_SCALE ** 2,
                                        ALU.add, ALU.mult).then_inc(n2_done, 1)

            def split_units(g):
                dve.wait_ge(rn_done, g + 1)
                dve.wait_ge(wh_copied, g + 1)
                since(dve, ut_done, g)
                for t in range(SUB):
                    row = Wh[:, ds(g * SUB + t, 1), :].rearrange("p o d -> p (o d)")
                    last = nc.vector.tensor_scalar(unit[:, 0, t, :], row, rnorm[:, t:t + 1], None, ALU.mult)
                last.then_inc(unit_hi, 1)
                dve.wait_ge(unit_hi, g + 1)
                for t in range(SUB):
                    row = Wh[:, ds(g * SUB + t, 1), :].rearrange("p o d -> p (o d)")
                    last = nc.vector.scalar_tensor_tensor(unit[:, 1, t, :], row, rnorm[:, t:t + 1],
                                                          unit[:, 0, t, :], ALU.mult, ALU.subtract)
                last.then_inc(unit_done, 1)

            def add_quarter(tile, r):
                if r == 0:
                    return
                dve.wait_ge(signed, quarter(tile, r))
                nc.vector.tensor_scalar(signs[:, r % 2, :], signs[:, r % 2, :], float(4 ** r), None,
                                        ALU.mult).then_inc(scaled, 1)
                dve.wait_ge(scaled, 4 * tile + r)
                since(dve, summed, 3 * tile + r - 1)
                if r == 1:
                    since(dve, packed, tile)
                all_sums = weighed[:, :, :].rearrange("p h w -> p (h w)")
                nc.vector.tensor_tensor(out=all_sums, in0=signs[:, 0, :] if r == 1 else all_sums,
                                        in1=signs[:, r % 2, :], op=ALU.add).then_inc(summed, 1)

            def finish_row(tile, slot):
                dve.wait_ge(summed, 3 * tile + 3)
                nc.vector.tensor_scalar(weighed[:, 1, :], weighed[:, 1, :], 2.0, None, ALU.mult).then_inc(scaled, 1)
                dve.wait_ge(scaled, 4 * tile + 4)
                nc.vector.tensor_tensor(out=row_words[:, ds(slot, 1), :].rearrange("p o w -> p (o w)"),
                                        in0=weighed[:, 0, :], in1=weighed[:, 1, :], op=ALU.add).then_inc(packed, 1)

            def quarter_words(tile, r):
                add_quarter(tile, r)
                if r == 3:
                    finish_row(tile, tile)

            copy_xt(0, 0)
            copy_xt(1, 1)
            for r in range(2):
                quarter_words(0, r)
            guard_norms(0)

            def two_groups(i):
                for odd in range(2):
                    g = 2 * i + 1 + odd
                    copy_xt(g + 1, odd)
                    split_units(g - 1)
                    for r in range(2):
                        quarter_words(i + odd, 2 - 2 * odd + r)
                    guard_norms(g)

            two_groups(0)
            with dve.Fori(1, NS // 2 - 1) as i:
                two_groups(i)
            dve.wait_ge(wc_in, 16 * 6)
            dve.wait_ge(consts, 1)
            for k in range(2 * KD):
                last = nc.vector.tensor_scalar(bcast[:, k, :], ident32[:], 0.0, bcol[:, k:k + 1], ALU.mult, ALU.add)
            last.then_inc(bc_done, 1)
            split_units(NS - 2)
            quarter_words(SUB - 1, 2)
            guard_norms(NS - 1)
            dve.wait_ge(sq_done, NS)
            nc.vector.tensor_reduce(out=big[:, 0:1], in_=norm2[:], op=ALU.max, axis=AX.X).then_inc(top_done, 1)
            dve.wait_ge(top_done, 1)
            nc.vector.tensor_scalar(big[:, 0:1], big[:, 0:1], EPS_SIM, None, ALU.add).then_inc(max_done, 1)
            split_units(NS - 1)
            quarter_words(SUB - 1, 3)
            dve.wait_ge(fused, 1)
            nc.vector.tensor_tensor(out=bias[:], in0=ps[:, 4, 0:D], in1=bcomb_in, op=ALU.add).then_inc(
                fused_copied, 1)

            dve.wait_ge(scale_done, 1)
            nc.vector.tensor_scalar(big[:, 2:3], big[:, 2:3], VAL_TOP, None, ALU.mult)
            nc.vector.tensor_scalar(big[:, 3:4], big[:, 3:4], 1.0 / VAL_TOP, None, ALU.mult).then_inc(vscale_done, 1)
            dve.wait_ge(vscale_done, 1)

            def low_values(k):
                for at, g in value_groups(k):
                    dve.wait_ge(vh_done, at + 1)
                    nc.vector.scalar_tensor_tensor(values[:, g * SUB:(g + 1) * SUB, LOW:LOW + D],
                                                   Wh[:, g * SUB:(g + 1) * SUB, :], big[:, 2:3],
                                                   values[:, g * SUB:(g + 1) * SUB, 0:D],
                                                   ALU.mult, ALU.subtract).then_inc(vl_done, 1)

            low_values(0)

            def unpack(s, c, k):
                n = unit_at(s, c, k)
                since(dve, masked, n - (UNITS - 1))
                w = words[:, s, ds(c, 1), :].rearrange("p a w -> p (a w)")
                for b in (2 * pair_of(k), 2 * pair_of(k) + 1):
                    last = nc.vector.tensor_scalar(mask[:, b, :], w, 14 - b, 0x4000,
                                                   ALU.logical_shift_left, ALU.bitwise_and)
                last.then_inc(unpacked, 1)
                if s // 2 == pair_of(k):
                    dve.wait_ge(unpacked, n + 1)
                    own = mask16[:, s, ds(c * P, P)]
                    nc.vector.tensor_tensor(out=own, in0=own, in1=diag2[:], op=ALU.max).then_inc(diag_done, 1)

            def unit_low(s, c, k):
                kks = computed(s, k)
                if not kks:
                    return
                dve.wait_ge(highs, computed_before(s, c, k) + 1)
                split = exps_split[:, k % 2, kks[0]:2, :, :, :].rearrange("p k t h n -> p (k t) h n")
                z = sim_ps[k % 2][:, kks[0] * SW:2 * SW].rearrange("p (t n) -> p t n", n=P)
                nc.vector.tensor_tensor(out=split[:, :, 1, :], in0=z, in1=split[:, :, 0, :],
                                        op=ALU.subtract).then_inc(lows, 1)

            def unit_mask(s, c, k):
                n = unit_at(s, c, k)
                dve.wait_ge(unpacked, n + 1)
                if s // 2 == pair_of(k):
                    dve.wait_ge(diag_done, NC * s + c + 1)
                since(dve, attended, n - (UNITS - 1))
                for kk in mirrored(s, k):
                    b = 2 * pair_of(k) + kk
                    dve.wait_ge(mirror_ready[b], 16 * (NC * (s - b - 1) + c + 1))
                    for h, dst in enumerate((Ph, Pl)):
                        last = nc.vector.tensor_tensor(out=dst[:, k, kk, :], in0=mirror_in[:, k % 2, kk, h, :],
                                                       in1=mask16[:, 2 * pair_of(k) + kk, :], op=ALU.mult)
                kks = computed(s, k)
                if kks:
                    dve.wait_ge(lows, computed_before(s, c, k) + 1)
                    b = 2 * pair_of(k)
                    m = mask16[:, b + kks[0]:b + 2, :].rearrange("p k (t n) -> p (k t) n", n=P)
                    split = exps_split[:, k % 2, kks[0]:2, :, :, :].rearrange("p k t h n -> p (k t) h n")
                    for h, dst in enumerate((Ph, Pl)):
                        last = nc.vector.tensor_tensor(
                            out=dst[:, k, kks[0]:2, :].rearrange("p k (t n) -> p (k t) n", n=P),
                            in0=split[:, :, h, :], in1=m, op=ALU.mult)
                last.then_inc(masked, 1)

            def read_attention(s):
                dve.wait_ge(attended, UPS * (s + 1))
                dve.wait_ge(x_in, 16 * NC)
                since(dve, attn_read, SUB * s)
                since(dve, ln_done, s)
                nc.vector.reciprocal(rsum[:], out_ps[:, :, D]).then_inc(rs_done, 1)
                dve.wait_ge(rs_done, s + 1)
                nc.vector.tensor_scalar(rsum[:], rsum[:], big[:, 3:4], None, ALU.mult).then_inc(rs_scaled, 1)
                dve.wait_ge(rs_scaled, s + 1)
                for t in range(SUB):
                    row = X[:, ds(SUB * s + t, 1), :].rearrange("p o d -> p (o d)")
                    nc.vector.scalar_tensor_tensor(mixed[:, t, :], out_ps[:, t, 0:D], rsum[:, t:t + 1], row,
                                                   ALU.mult, ALU.add).then_inc(attn_read, 1)

            def moments_of(tiles, at):
                since(dve, ln_done, at)
                for t in range(SUB):
                    last = nc.vector.bn_stats(stats[:, t, :], tiles(t))
                last.then_inc(st_done, 1)
                dve.wait_ge(st_done, at + 1)
                even, odd = stats[:, :, 0:3], stats[:, :, 3:6]
                nc.vector.tensor_tensor(out=mean_sum[:], in0=even[:, :, 1], in1=odd[:, :, 1], op=ALU.add)
                nc.vector.tensor_tensor(out=mean_gap[:], in0=even[:, :, 1], in1=odd[:, :, 1], op=ALU.subtract)
                nc.vector.tensor_tensor(out=squares[:], in0=even[:, :, 2], in1=odd[:, :, 2],
                                        op=ALU.add).then_inc(parts_done, 1)
                dve.wait_ge(parts_done, 2 * at + 1)
                nc.vector.tensor_scalar(mean[:], mean_sum[:], 0.5, None, ALU.mult)
                nc.vector.tensor_tensor(out=gap2[:], in0=mean_gap[:], in1=mean_gap[:], op=ALU.mult)
                nc.vector.tensor_scalar(squares[:], squares[:], 1.0 / D, EPS_LN, ALU.mult, ALU.add).then_inc(
                    parts_done, 1)
                dve.wait_ge(parts_done, 2 * at + 2)
                nc.vector.scalar_tensor_tensor(rstd[:], gap2[:], 0.25, squares[:], ALU.mult, ALU.add).then_inc(
                    var_done, 1)

            def normalise(dst, tiles, at):
                dve.wait_ge(rstd_done, at + 1)
                for t in range(SUB):
                    last = nc.vector.tensor_scalar(dst(t), tiles(t), mean[:, t:t + 1], rstd[:, t:t + 1],
                                                   ALU.subtract, ALU.mult)
                last.then_inc(ln_done, 1)

            def x_tile(s):
                return lambda t: X[:, ds(SUB * s + t, 1), :].rearrange("p o d -> p (o d)")

            def mixed_tile(t):
                return mixed[:, t, :]

            def iteration(s, c, c0, finish):
                for k in range(UNITS):
                    if finish and k == 0:
                        dve.wait_ge(words_first, s + 1)
                    unpack(s, c, k)
                    if finish and k == 0:
                        nc.vector.tensor_scalar(words[:, s, 1:NC, :].rearrange("p c w -> p (c w)"),
                                                word_ps[:, SW:NC * SW], 0.5, WORD_BIAS,
                                                ALU.mult, ALU.add).then_inc(words_rest, 1)
                    unit_low(s, c, k)
                    unit_mask(s, c, k)
                    for tile, q in quarters_packed(s, c, c0, k):
                        add_quarter(tile, q)
                        if q == 3:
                            finish_row(tile, tile - slot_base(s, c0, tile))
                    if finish and s > 0 and k == LEAD - 2:
                        read_attention(s - 1)
                    if finish and s > 0 and k == UNITS - 2:
                        dve.wait_ge(attn_read, SUB * s)
                        moments_of(mixed_tile, s - 1)
                    if finish and s > 0 and k == UNITS - 1:
                        normalise(x_tile(s - 1), mixed_tile, s - 1)
                    if finish and s == 0 and k + 1 < UNITS:
                        low_values(k + 1)

            def slot_base(s, c0, tile):
                t = tile if isinstance(tile, int) else tiles_packed(s, c0, c0)[0]
                return t - t % RING

            def low_x1(c, b1, at):
                dve.wait_ge(x1_hi, at)
                place = x1c[:, ds(c, 1), 0:b1, :].rearrange("p o b w -> p (o b) w")
                nc.vector.scalar_tensor_tensor(place[:, :, LOW:LOW + D],
                                               Xc[:, ds(c, 1), 0:b1, :].rearrange("p o b d -> p (o b) d"), X1_SCALE,
                                               place[:, :, 0:D], ALU.mult, ALU.subtract).then_inc(x1_split, 1)

            def last_iteration(c, c0):
                iteration(NS - 1, c, c0, False)
                low_x1(c - 1, BITS - 1, c)

            for s in range(NS):
                iteration(s, 0, 0, True)
                if s == 0:
                    dve.wait_ge(msq_done, 1)
                    nc.vector.tensor_reduce(out=mscale[:, 0:1], in_=msum[:], op=ALU.max, axis=AX.X).then_inc(m_steps, 1)
                    dve.wait_ge(m_steps, 1)
                    nc.vector.tensor_scalar(mscale[:, 0:1], mscale[:, 0:1], EPS_M, None, ALU.add).then_inc(msum_done, 1)
                over_c(dve, s, last_iteration if s == NS - 1 else lambda c, c0: iteration(s, c, c0, False))

            def unpack_late(s, c, bs=range(BITS), used=None):
                w = words[:, ds(s, 1), ds(c, 1), :].rearrange("p o a w -> p (o a w)")
                for b in bs:
                    since(dve, mask_used, BITS * (NC * s + c - 1) + b + 1 if used is None else used)
                    nc.vector.tensor_scalar(mask[:, b, :], w, 14 - b, 0x4000,
                                            ALU.logical_shift_left, ALU.bitwise_and).then_inc(mask_ready, 1)

            dve.wait_ge(mpow_done, 1)
            nc.vector.tensor_scalar(mscale[:, 1:2], mscale[:, 1:2], VAL_TOP, None, ALU.mult)
            nc.vector.tensor_scalar(mscale[:, 3:4], mscale[:, 2:3], 1.0 / (VAL_TOP * X1_SCALE), None, ALU.mult)
            nc.vector.tensor_scalar(mscale[:, 0:1], mscale[:, 2:3], 1.0 / VAL_TOP, None,
                                    ALU.mult).then_inc(mscale_done, 1)
            dve.wait_ge(signed, 4 * NT)
            nc.vector.tensor_reduce(out=rdeg[:], in_=degree[:], op=ALU.add, axis=AX.X).then_inc(deg_sum, 1)
            dve.wait_ge(deg_sum, 1)
            nc.vector.tensor_scalar(rdeg[:], rdeg[:], 0.5, N / 2.0, ALU.mult, ALU.add).then_inc(deg_max, 1)
            dve.wait_ge(deg_max, 1)
            nc.vector.tensor_scalar(rdeg[:], rdeg[:], 1.0, None, ALU.max).then_inc(deg_max, 1)
            dve.wait_ge(deg_max, 2)
            nc.vector.reciprocal(rdeg[:], rdeg[:]).then_inc(rdeg_done, 1)
            dve.wait_ge(rdeg_done, 1)
            dve.wait_ge(mscale_done, 1)
            nc.vector.tensor_scalar(rdeg[:], rdeg[:], mscale[:, 0:1], None, ALU.mult).then_inc(rdeg_done, 1)
            dve.wait_ge(masked, UPS * NS)
            unpack_late(0, 0)

            read_attention(NS - 1)
            dve.wait_ge(attn_read, SUB * NS)
            moments_of(mixed_tile, NS - 1)
            unpack_late(0, 1, range(BITS // 2))
            normalise(x_tile(NS - 1), mixed_tile, NS - 1)
            unpack_late(0, 1, range(BITS // 2, BITS - 1))
            dve.wait_ge(ln_done, NS)
            dve.wait_ge(x1_hi, NC + 1)
            nc.vector.scalar_tensor_tensor(x1s[:, NT - SUB:NT, LOW:LOW + D], X[:, NT - SUB:NT, :], X1_SCALE,
                                           x1s[:, NT - SUB:NT, 0:D], ALU.mult, ALU.subtract).then_inc(x1_split, 1)
            low_x1(NC - 1, BITS - 1, NC)
            unpack_late(0, 1, [BITS - 1], 2 * BITS - 1)
            unpack_late(0, 2)
            dve.wait_ge(m_hi, 1)
            for i, M in enumerate((M1, M2)):
                last = nc.vector.scalar_tensor_tensor(Ms[:, i, 1, :, :], M[:, :, :], mscale[:, 1:2],
                                                      Ms[:, i, 0, :, :], ALU.mult, ALU.subtract)
            last.then_inc(m_split, 1)
            unpack_late(0, 3)

            def keep_aggregate(s):
                dve.wait_ge(mask_used, BITS * NC * (s + 1))
                since(dve, feat_done, SUB * s)
                unscale = 1.0 / (MASK_ONE * X1_SCALE)
                nc.vector.tensor_scalar(aggT[:, 0, 1, :], ps[:, 1, :], unscale, None, ALU.mult).then_inc(agg_hi1, 1)
                dve.wait_ge(agg_hi, s + 1)
                nc.vector.scalar_tensor_tensor(aggT[:, 1, 0, :], ps[:, 0, :], unscale, aggT[:, 0, 0, :],
                                               ALU.mult, ALU.subtract)
                dve.wait_ge(agg_hi1, s + 1)
                nc.vector.scalar_tensor_tensor(aggT[:, 1, 1, :], ps[:, 1, :], unscale, aggT[:, 0, 1, :],
                                               ALU.mult, ALU.subtract).then_inc(agg_copied, 1)

            def bias_features(s):
                dve.wait_ge(own_done, s + 1)
                since(dve, ln_done, NS + s)
                nc.vector.scalar_tensor_tensor(feat, ps[:, 4:8, 0:D], mscale[:, 3:4],
                                               bias[:].rearrange("p (o d) -> p o d", o=1).broadcast_to([P, SUB, D]),
                                               ALU.mult, ALU.add).then_inc(feat_b, 1)

            def sum_features(s):
                dve.wait_ge(feat_b, s + 1)
                for t in range(SUB + 1):
                    if t < SUB:
                        dve.wait_ge(feat_done, SUB * s + t + 1)
                        nc.vector.scalar_tensor_tensor(feat[:, t, :], ps[:, 4 + t, D:2 * D],
                                                       rdeg[:, ds(SUB * s + t, 1)], feat[:, t, :],
                                                       ALU.mult, ALU.add).then_inc(feat_sum, 1)
                    if t > 0:
                        dve.wait_ge(feat_sum, SUB * s + t)
                        last = nc.vector.scalar_tensor_tensor(feat[:, t - 1, :], feat[:, t - 1, :], 0.0,
                                                              X[:, ds(SUB * s + t - 1, 1), :].rearrange("p o d -> p (o d)"),
                                                              ALU.max, ALU.add)
                last.then_inc(feat_res, 1)

            def finish_features(s):
                dve.wait_ge(feat_res, s + 1)
                moments_of(lambda t: feat[:, t, :], NS + s)
                since(dve, stored, 16 * s)
                normalise(lambda t: result[:, t, :], lambda t: feat[:, t, :], NS + s)

            keep_aggregate(0)
            def layer_tile(s):
                unpack_late(s, 0)
                bias_features(s - 1)
                unpack_late(s, 1)
                sum_features(s - 1)
                unpack_late(s, 2)
                finish_features(s - 1)
                unpack_late(s, 3)
                keep_aggregate(s)

            layer_tile(1)
            with dve.Fori(2, NS) as s:
                layer_tile(s)
            bias_features(NS - 1)
            sum_features(NS - 1)
            finish_features(NS - 1)


_INS = ['x', 'adj', 'L0_gnn_W', 'L1_gnn_W_self', 'L1_gnn_b_self', 'L1_gnn_W_nb', 'L1_gnn_b_nb',
        'L1_gnn_W_comb', 'L1_gnn_b_comb']


def kernel(**inputs):
    import numpy as _np
    import concourse.bacc as _bacc
    from concourse import mybir as _mybir
    from concourse.bass_utils import run_bass_kernel_spmd as _run

    nc = _bacc.Bacc("TRN2", target_bir_lowering=False, num_devices=1)
    arrays, args = {}, []
    for name in _INS:
        a = _np.ascontiguousarray(inputs[name])
        arrays[f"in_{name}_dram"] = a
        args.append(nc.dram_tensor(f"in_{name}_dram", a.shape, _mybir.dt.from_np(a.dtype), kind="ExternalInput").ap())
    args.append(nc.dram_tensor("out_0_dram", (N, D), _mybir.dt.float32, kind="ExternalOutput").ap())
    gnn_kernel(nc, *args)
    r = _run(nc, [arrays], core_ids=[0])
    return r.results[0]["out_0_dram"]
```
